# Optimizing a Trainium2 kernel written in Bass

```python
import numpy as np
import jax
import jax.numpy as jnp

def _softmax(x, axis=-1):
    return jax.nn.softmax(x, axis=axis)

def _gelu(x):
    return jax.nn.gelu(x, approximate=True)

def _silu(x):
    return jax.nn.silu(x)

def _sigmoid(x):
    return jax.nn.sigmoid(x)

def _layernorm(x, axis=-1, eps=1e-05):
    m = jnp.mean(x, axis=axis, keepdims=True)
    v = jnp.var(x, axis=axis, keepdims=True)
    return (x - m) / jnp.sqrt(v + eps)

def _scatter_add(tgt, idx, src, axis=0):
    return tgt.at[idx].add(src)

def _segment_sum(src, seg, n):
    return jax.ops.segment_sum(src, seg, n)
kernel_name = 'mk_flamingo_gated_d1_seqx_r8_3311a6'

def setup_inputs(seed: int=0):
    np.random.seed(seed)
    _w = jnp.asarray

    def _rec_inputs():
        import jax
        import jax.numpy as jnp
        _rk = jax.random.key(seed)
        x = -0.0002928 + 1 * jax.random.normal(jax.random.fold_in(_rk, 1), (128, 64, 128), jnp.float32)
        _lenS = 64 - jax.random.randint(jax.random.fold_in(_rk, 7), (128,), 0, max(1, 64 // 4) + 1, jnp.int32)
        _lenS2 = 64 - jax.random.randint(jax.random.fold_in(_rk, 8), (128,), 0, max(1, 64 // 4) + 1, jnp.int32)
        _ctx_1024P = jax.random.normal(jax.random.fold_in(_rk, 11), (128, 16, 128), jnp.float32)
        _ctx_1024c = jax.random.dirichlet(jax.random.fold_in(_rk, 511), 0.3 * jnp.ones((16,), jnp.float32), (128, 64))
        _ctx_1024t = jnp.einsum('bsk,bkd->bsd', _ctx_1024c, _ctx_1024P)
        _ctx_1024t = _ctx_1024t * jax.lax.rsqrt(jnp.mean(jnp.square(_ctx_1024t)) + 1e-12) * 0.953939
        ctx_1024 = -1.39393e-06 + 0.999914 * (_ctx_1024t + 0.3 * jax.random.normal(jax.random.fold_in(_rk, 611), (128, 64, 128), jnp.float32))
        _g = jax.random.normal(jax.random.fold_in(_rk, 9001), (2, 1), jnp.float32)
        _g = jnp.sign(_g) * jnp.maximum(jnp.abs(_g), 1.0) + (_g == 0) * 1.0
        g_xattn = _g[0]
        g_ffn = _g[1]
        return (x, ctx_1024, g_xattn, g_ffn)
    x, ctx_1024, g_xattn, g_ffn = _rec_inputs()

    def _L0_xattn_setup():
        import jax, jax.numpy as jnp
        import numpy as np
        DIM, HEADS, DEPTH, SEQ, LOCAL_W = (128, 16, 7, 256, 64)
        HEAD_DIM = DIM // HEADS
        SCALE = 1.0 / HEAD_DIM ** 0.5

        def cantor_mask(S, depth, local_window):
            idx = np.arange(S)
            d = np.abs(idx[:, None] - idx[None, :])
            x = d.copy()
            ok = np.ones_like(d, dtype=bool)
            for _ in range(depth):
                ok &= x % 3 != 1
                x //= 3
            ok &= x == 0
            return jnp.asarray(ok | (d <= local_window))
        key = jax.random.key(seed)
        ks = jax.random.split(key, 8)
        B = 2
        s = 0.02
        return {'query': jax.random.normal(ks[0], (B, SEQ, DIM), jnp.float32), 'key_value': jax.random.normal(ks[1], (B, SEQ, DIM), jnp.float32), 'Wq': jax.random.normal(ks[2], (DIM, DIM), jnp.float32) * s, 'bq': jnp.zeros((DIM,), jnp.float32), 'Wkv': jax.random.normal(ks[3], (DIM, 2 * DIM), jnp.float32) * s, 'bkv': jnp.zeros((2 * DIM,), jnp.float32), 'Wo': jax.random.normal(ks[4], (DIM, DIM), jnp.float32) * s, 'bo': jnp.zeros((DIM,), jnp.float32)}
    _L0_xattn_all = _L0_xattn_setup()
    _L0_xattn_in = {k: v for k, v in _L0_xattn_all.items() if k in ('Wq', 'bq', 'Wkv', 'bkv', 'Wo', 'bo')}
    del _L0_xattn_all

    def _L0_ffn_setup():
        import jax, jax.numpy as jnp
        import numpy as np
        TOPK = 2
        key = jax.random.key(seed)
        k0, k1, k2, k3, k4 = jax.random.split(key, 5)
        B, S, D, E, H = (4, 256, 128, 8, 352)
        return {'x': jax.random.normal(k0, (B, S, D), dtype=jnp.float32), 'gate_w': jax.random.normal(k1, (E, D), dtype=jnp.float32) * 0.02, 'w1': jax.random.normal(k2, (E, H, D), dtype=jnp.float32) * 0.02, 'w2': jax.random.normal(k3, (E, D, H), dtype=jnp.float32) * 0.02, 'w3': jax.random.normal(k4, (E, H, D), dtype=jnp.float32) * 0.02}
    _L0_ffn_all = _L0_ffn_setup()
    _L0_ffn_in = {k: v for k, v in _L0_ffn_all.items() if k in ('gate_w', 'w1', 'w2', 'w3')}
    del _L0_ffn_all
    return {'x': x, 'ctx_1024': ctx_1024, 'g_xattn': g_xattn, 'g_ffn': g_ffn, 'L0_xattn_Wq': _L0_xattn_in['Wq'], 'L0_xattn_bq': _L0_xattn_in['bq'], 'L0_xattn_Wkv': _L0_xattn_in['Wkv'], 'L0_xattn_bkv': _L0_xattn_in['bkv'], 'L0_xattn_Wo': _L0_xattn_in['Wo'], 'L0_xattn_bo': _L0_xattn_in['bo'], 'L0_ffn_gate_w': _L0_ffn_in['gate_w'], 'L0_ffn_w1': _L0_ffn_in['w1'], 'L0_ffn_w2': _L0_ffn_in['w2'], 'L0_ffn_w3': _L0_ffn_in['w3']}

def reference(x, ctx_1024, g_xattn, g_ffn, L0_xattn_Wq, L0_xattn_bq, L0_xattn_Wkv, L0_xattn_bkv, L0_xattn_Wo, L0_xattn_bo, L0_ffn_gate_w, L0_ffn_w1, L0_ffn_w2, L0_ffn_w3):
    import jax
    import jax.numpy as jnp

    def _L0_xattn_ref(query, key_value, Wq, bq, Wkv, bkv, Wo, bo):
        import jax, jax.numpy as jnp
        import numpy as np
        DIM, HEADS, DEPTH, SEQ, LOCAL_W = (128, 16, 7, 256, 64)
        HEAD_DIM = DIM // HEADS
        SCALE = 1.0 / HEAD_DIM ** 0.5

        def cantor_mask(S, depth, local_window):
            idx = np.arange(S)
            d = np.abs(idx[:, None] - idx[None, :])
            x = d.copy()
            ok = np.ones_like(d, dtype=bool)
            for _ in range(depth):
                ok &= x % 3 != 1
                x //= 3
            ok &= x == 0
            return jnp.asarray(ok | (d <= local_window))
        B, S, D = query.shape
        H, hd = (HEADS, HEAD_DIM)
        mask = cantor_mask(S, DEPTH, LOCAL_W)
        q = (query @ Wq + bq).reshape(B, S, H, hd).transpose(0, 2, 1, 3)
        kv = (key_value @ Wkv + bkv).reshape(B, S, 2, H, hd).transpose(2, 0, 3, 1, 4)
        k, v = (kv[0], kv[1])
        scores = jnp.einsum('bhqd,bhkd->bhqk', q, k) * SCALE
        scores = jnp.where(mask, scores, jnp.finfo(scores.dtype).min)
        attn = jax.nn.softmax(scores, axis=-1)
        out = jnp.einsum('bhqk,bhkd->bhqd', attn, v)
        out = out.transpose(0, 2, 1, 3).reshape(B, S, D)
        return out @ Wo + bo

    def _L0_ffn_ref(x, gate_w, w1, w2, w3):
        import jax, jax.numpy as jnp
        import numpy as np
        TOPK = 2
        B, S, D = x.shape
        E = gate_w.shape[0]
        T = B * S
        xf = x.reshape(T, D)
        logits = xf @ gate_w.T
        tw, ti = jax.lax.top_k(logits, TOPK)
        tw = jax.nn.softmax(tw, axis=-1)
        cw = jnp.zeros((T, E), dtype=xf.dtype).at[jnp.arange(T)[:, None], ti].add(tw)
        out = jnp.zeros_like(xf)
        for e in range(E):
            h = jax.nn.silu(xf @ w1[e].T) * (xf @ w3[e].T)
            out = out + cw[:, e:e + 1] * (h @ w2[e].T)
        return out.reshape(B, S, D)
    x = x + jnp.tanh(g_xattn[0]) * _L0_xattn_ref(_layernorm(x, axis=-1), ctx_1024, L0_xattn_Wq, L0_xattn_bq, L0_xattn_Wkv, L0_xattn_bkv, L0_xattn_Wo, L0_xattn_bo)
    x = x + jnp.tanh(g_ffn[0]) * _L0_ffn_ref(_layernorm(x, axis=-1), L0_ffn_gate_w, L0_ffn_w1, L0_ffn_w2, L0_ffn_w3)
    return x

_drawn_inputs = setup_inputs


def setup_inputs(seed=0):
    import zlib

    import numpy as np

    out = dict(_drawn_inputs(seed))
    spreads = {'L0_xattn_bq': (0.0, 0.8), 'L0_xattn_bkv': (0.0, 0.509), 'L0_xattn_bo': (0.0, 0.1)}
    factors = {'ctx_1024': 3.192,
     'L0_xattn_Wq': 8.0,
     'L0_xattn_Wkv': 2.807,
     'L0_ffn_gate_w': 8.0,
     'L0_ffn_w1': 8.0,
     'L0_ffn_w2': 8.0,
     'L0_ffn_w3': 8.0}
    for name, (base, spread) in spreads.items():
        noise = np.random.default_rng([zlib.crc32(name.encode()), seed]).standard_normal(out[name].shape)
        drawn = base * np.exp(spread * noise) if base else spread * noise
        out[name] = jnp.asarray(drawn.astype(out[name].dtype))
    for name, factor in factors.items():
        out[name] = (out[name] * factor).astype(out[name].dtype)
    return out
```

```python
from contextlib import ExitStack

import concourse.bass as bass
from concourse import mybir

FP32 = mybir.dt.float32
FP32R = mybir.dt.float32r
U32 = mybir.dt.uint32
I32 = mybir.dt.int32
ALU = mybir.AluOpType
ACT = mybir.ActivationFunctionType
AX = mybir.AxisListType

B, S, D = 128, 64, 128
HEADS = 16
HD = D // HEADS
P = 128
TOKENS = B * S
PAIRS = TOKENS // P
PG = 4
GROUPS = PAIRS // PG
QUAD = 4
EPS = 1e-5
UNROLL1, UNROLL2, UNROLL3, UNROLL4 = 2, 8, 4, 2
VB = 2 * 2 * (HD + 1)

E, H, TOPK = 8, 352, 2
CHUNKS = 3
HP = CHUNKS * P
REGION = TOKENS + P
NULL_ROW = E * REGION
ROW = D + 4
TRASH = TOPK * TOKENS
TILES = TOPK * TOKENS // P + E
BELOW_ALL = -3e38
MAGIC = 0x5F3759DF

C_IDENT, C_TRI, C_ONES = 0, P, 2 * P
C_HEAD = 3 * P
C_BATCH = C_HEAD + QUAD
C_PARITY = C_BATCH + 2
C_EPS = C_PARITY + 2
C_RANK = C_EPS + 1
C_REGION = C_RANK + E
C_DEST = C_REGION + E
C_PART = C_DEST + PG * TOPK
C_TRASH = C_PART + 1
C_TILE = C_TRASH + 2 * E
C_END = C_TILE + TILES


def build(nc, x, ctx, consts, qk_bias, gates, bv, bo, w_qkv, w_o, w_gate, w13, w2, out):
    es = ExitStack()
    with es:
        sb = lambda name, shape, dt=FP32: es.enter_context(nc.sbuf_tensor(name, shape, dt))
        sem = lambda name: es.enter_context(nc.semaphore(name))
        pair_of = lambda make: [make(0), make(1)]

        const_sb = sb("const_sb", [P, C_END])
        const = lambda at, n=1: const_sb[:, at:at + n]
        ident, tri, ones = const(C_IDENT, P), const(C_TRI, P), const(C_ONES, P)
        head_mask = const(C_HEAD, QUAD)
        batch_mask = const(C_BATCH, 2)
        parity_mask = const(C_PARITY, 2)
        ident_r = sb("ident_r", [P, P], FP32R)
        bias_sb = sb("bias_sb", [P, 4])
        gate_sb = sb("gate_sb", [P, 2])
        tanh_gate = sb("tanh_gate", [P, 2])
        bv_sb = sb("bv_sb", [P, 1])
        bo_sb = sb("bo_sb", [1, D])
        wqkv_sb = sb("wqkv_sb", [P, 3 * D])
        wo_sb = sb("wo_sb", [P, D])
        wgate_sb = sb("wgate_sb", [P, E])
        w2_sb = sb("w2_sb", [P, CHUNKS * E * D])

        k_all = sb("k_all", [P, PAIRS * 2 * S])
        qx_all = sb("qx_all", [P, PAIRS * 2 * S])
        v_all = sb("v_all", [P, PAIRS * 2 * D])
        w13_sb = k_all[:, 0:E * 2 * H]

        arena = sb("arena", [P, 4096])
        x_in = pair_of(lambda s: arena[:, 512 * s:512 * s + 512])
        c_in = pair_of(lambda s: arena[:, 1024 + 512 * s:1536 + 512 * s])
        xn_t = pair_of(lambda s: arena[:, 2048 + 512 * s:2560 + 512 * s])
        c_t = pair_of(lambda s: arena[:, 3072 + 512 * s:3584 + 512 * s])
        probs = pair_of(lambda s: arena[:, 1024 * s:1024 * s + 1024])
        probs_t = pair_of(lambda s: arena[:, 2048 + 1024 * s:3072 + 1024 * s])
        k_mask = pair_of(lambda s: sb(f"k_mask{s}", [P, 2, QUAD, S]))
        q_blk = pair_of(lambda s: sb(f"q_blk{s}", [P, 2, 2, S]))
        v_blk = pair_of(lambda s: sb(f"v_blk{s}", [P, HEADS // 2 * VB]))
        neg_max = pair_of(lambda s: sb(f"neg_max{s}", [P, HEADS], FP32R))
        rsum = sb("rsum", [P, HEADS])
        o_buf = pair_of(lambda s: sb(f"o_buf{s}", [P, D]))
        o_t = pair_of(lambda s: sb(f"o_t{s}", [P, D]))
        x_res = pair_of(lambda s: sb(f"x_res{s}", [P, D]))
        stats = sb("stats", [P, PG, 6])
        mv = sb("mv", [P, PG, 2])
        std = sb("std", [P, PG])
        rstd = sb("rstd", [P, PG])
        var = sb("var", [P, PG])
        newton = sb("newton", [P, PG])
        x2g = pair_of(lambda s: sb(f"x2g{s}", [P, PG, D]))
        xn2_t = pair_of(lambda s: sb(f"xn2_t{s}", [P, D]))
        logits = pair_of(lambda s: sb(f"logits{s}", [P, PG, E]))
        best = sb("best", [P, PG])
        second = sb("second", [P, PG])
        picked = sb("picked", [P, PG])
        rest = sb("rest", [P, PG, E])
        work = sb("work", [P, TOPK, PG, E])
        chosen = sb("chosen", [P, TOPK, PG, E])
        either = sb("either", [P, PG, E])
        gap = sb("gap", [P, PG])
        ratio = sb("ratio", [P, PG])
        share = sb("share", [P, PG])
        place = sb("place", [P, PG, E])
        place_of = sb("place_of", [P, TOPK, PG])
        index = pair_of(lambda s: sb(f"index{s}", [P, TOPK, PG], U32))
        base = sb("base", [P, E])
        dest = sb("dest", [P, PG, TOPK])
        rows = pair_of(lambda s: sb(f"rows{s}", [P, PG, TOPK, ROW]))
        pad_rows = sb("pad_rows", [P, 2 * E, ROW])
        pad_place = sb("pad_place", [P, E])
        pad_index = sb("pad_index", [P, E], U32)

        count = sb("count", [P, E])
        count_i = sb("count_i", [P, E], I32)
        tiles_of = sb("tiles_of", [P, E])
        upto = pair_of(lambda s: sb(f"upto{s}", [P, E]))
        skip = sb("skip", [P, E])
        passed = v_all[0:1, 0:TILES * E].rearrange("p (t e) -> p t e", e=E)
        skipped = v_all[0:1, TILES * E:2 * TILES * E].rearrange("p (t e) -> p t e", e=E)
        tile_f = sb("tile_f", [1, 2, TILES])
        tile_row = sb("tile_row", [1, TILES], I32)
        tile_expert = sb("tile_expert", [1, TILES], I32)

        at3 = [2 * TILES * E]

        def old(n):
            at3[0] += n
            return v_all[:, at3[0] - n:at3[0]]

        row_in = [old(ROW) for _ in range(4)]
        xt = pair_of(lambda s: old(D))
        gated = pair_of(lambda s: old(H))
        hidden = pair_of(lambda s: old(HP))
        hidden_t = pair_of(lambda s: old(HP))
        y_out = [old(D) for _ in range(4)]
        y_index = [sb(f"y_index{s}", [P, 1], U32) for s in range(4)]
        y_in = pair_of(lambda s: old(PG * TOPK * D))

        sorted_rows = nc.dram_tensor("sorted_rows", (NULL_ROW + E * P, ROW), FP32, kind="Internal").ap()
        expert_out = nc.dram_tensor("expert_out", (TRASH + 2 * E * P, D), FP32, kind="Internal").ap()

        bank = [es.enter_context(nc.psum_tensor(f"bank{i}", [P, 512], FP32)) for i in range(8)]
        scores = [bank[0:2], bank[2:4]]
        aux = bank[7]
        AUX_O, AUX_X, AUX_L, AUX_R, AUX_T = 0, 128, 256, 320, 384

        const_loaded, consts_ready, tanh_ready, bo_done = sem("const_loaded"), sem("consts_ready"), sem("tanh_ready"), sem("bo_done")
        w2_loaded, w13_loaded = sem("w2_loaded"), sem("w13_loaded")
        x_loaded, c_loaded = pair_of(lambda s: sem(f"x_loaded{s}")), pair_of(lambda s: sem(f"c_loaded{s}"))
        var_ready, std_ready, xn_ready = sem("var_ready"), sem("std_ready"), sem("xn_ready")
        xt_done, ct_done, xt_copied, ct_copied = sem("xt_done"), sem("ct_done"), sem("xt_copied"), sem("ct_copied")
        k_done, q_done, v_done = sem("k_done"), sem("q_done"), sem("v_done")
        k_copied, q_copied, v_copied = sem("k_copied"), sem("q_copied"), sem("v_copied")
        operands_ready, values_ready = sem("operands_ready"), sem("values_ready")
        scores_done, max_ready, shifted, probs_ready = sem("scores_done"), sem("max_ready"), sem("shifted"), sem("probs_ready")
        t_done, t_copied = pair_of(lambda h: sem(f"t_done{h}")), pair_of(lambda h: sem(f"t_copied{h}"))
        av_done, o_ready = sem("av_done"), sem("o_ready")
        res_loaded = pair_of(lambda s: sem(f"res_loaded{s}"))
        x2_ready = sem("x2_ready")
        mid_done, mid_read, end_done, end_read = sem("mid_done"), sem("mid_read"), sem("end_done"), sem("end_read")
        xn2_ready, gap_ready, ratio_ready, rows_copied, rows_ready = (
            sem("xn2_ready"), sem("gap_ready"), sem("ratio_ready"), sem("rows_copied"), sem("rows_ready"))
        scattered = pair_of(lambda s: sem(f"scattered{s}"))
        pads_ready, padded, table_ready = sem("pads_ready"), sem("padded"), sem("table_ready")
        row_loaded = [sem(f"row_loaded{s}") for s in range(4)]
        row_turned, row_copied, up_done, gated_ready, hidden_ready = (
            sem("row_turned"), sem("row_copied"), sem("up_done"), sem("gated_ready"), sem("hidden_ready"))
        hidden_turned, hidden_copied, down_done, y_ready = sem("hidden_turned"), sem("hidden_copied"), sem("down_done"), sem("y_ready")
        y_sent = [sem(f"y_sent{s}") for s in range(4)]
        y_loaded, sum_ready = pair_of(lambda s: sem(f"y_loaded{s}")), sem("sum_ready")
        stored, wait_carried = sem("stored"), sem("wait_carried")

        x_v = x.rearrange("(n c) s d -> (c s) n d", c=2)
        c_v = ctx.rearrange("(n c) s d -> (c s) n d", c=2)
        out_v = out.rearrange("(n c) s d -> (c s) n d", c=2)
        y_v = expert_out[0:TRASH, :].rearrange("(n p k) d -> p n k d", p=P, k=TOPK)

        class Sweep:

            def __init__(self, units, unroll, peeled):
                self.units, self.unroll, self.peeled = units, unroll, peeled

            def __call__(self, eng, lag, step):
                assert lag <= self.peeled * self.unroll
                for m in range(self.peeled * self.unroll):
                    step(m // self.unroll, m % self.unroll)
                with eng.Fori(self.peeled, self.units // self.unroll) as i:
                    for j in range(self.unroll):
                        step(i, j)
                for m in range(self.units, self.units + lag):
                    step(m // self.unroll, m % self.unroll)

            def live(self, i, j, lag=0):
                return not isinstance(i, int) or 0 <= i * self.unroll + j - lag < self.units

            def reached(self, i, j, unit):
                assert isinstance(i, int) or self.peeled * self.unroll + j >= unit
                return not isinstance(i, int) or i * self.unroll + j >= unit

        project, attend = Sweep(GROUPS, UNROLL1, 1), Sweep(PAIRS, UNROLL2, 3)
        experts, combine = Sweep(TILES, UNROLL3, 2), Sweep(GROUPS, UNROLL4, 1)

        def blocks(v):
            return v[:, :].rearrange("p (m h e) -> p m h e", h=2, e=HD + 1)

        N_CONST = 9 * 16
        ATTN_LAST = PAIRS + 9

        block = es.enter_context(nc.Block())

        @block.sync
        def _(sp):
            for dst, src in ((const_sb[:, :], consts), (bias_sb[:, :], qk_bias), (gate_sb[:, :], gates), (bv_sb[:, :], bv),
                             (bo_sb[:, :], bo), (wqkv_sb[:, :], w_qkv), (wo_sb[:, :], w_o), (wgate_sb[:, :], w_gate)):
                sp.dma_start(dst, src).then_inc(const_loaded, 16)
            sp.dma_start(w2_sb[:, :], w2).then_inc(const_loaded, 16)

            def load_step(i, j):
                s, n = j % 2, i * UNROLL1 + j
                if project.reached(i, j, 2):
                    sp.wait_ge(xt_done, n - 1)
                sp.dma_start(x_in[s].rearrange("p (q d) -> p q d", q=PG), x_v[:, bass.ds(n * PG, PG), :]).then_inc(x_loaded[s], 16)
                if project.reached(i, j, 2):
                    sp.wait_ge(ct_done, n - 1)
                sp.dma_start(c_in[s].rearrange("p (q d) -> p q d", q=PG), c_v[:, bass.ds(n * PG, PG), :]).then_inc(c_loaded[s], 16)

            project(sp, 0, load_step)

            def residual_step(i, j):
                s, n = j % 2, i * UNROLL2 + j
                if attend.reached(i, j, 2):
                    sp.wait_ge(x2_ready, n - 1)
                sp.dma_start(x_res[s][:, :], x_v[:, bass.ds(n, 1), :].rearrange("p n d -> p (n d)")).then_inc(res_loaded[s], 16)

            attend(sp, 0, residual_step)
            sp.wait_ge(operands_ready, 2 * PAIRS)
            sp.dma_start(w13_sb, w13).then_inc(w13_loaded, 16)
            sp.wait_ge(table_ready, 1)
            for s in range(2):
                sp.wait_ge(scattered[s], GROUPS // 2 * PG * TOPK * 16)
            sp.wait_ge(padded, (E + 1) * 16)

            def row_step(i, j):
                t, s = i * UNROLL3 + j, j % 4
                if experts.reached(i, j, 4):
                    sp.wait_ge(hidden_ready, t - 3)
                row = sp.value_load(tile_row[0:1, bass.ds(t, 1)], min_val=0, max_val=NULL_ROW + (E - 1) * P)
                sp.dma_start(row_in[s], sorted_rows[bass.ds(row, P), :]).then_inc(row_loaded[s], 16)

            experts(sp, 0, row_step)
            for s in range(4):
                sp.wait_ge(y_sent[s], TILES // 4 * 16)

            def y_step(i, j):
                s = j % 2
                if combine.live(i, j):
                    n = i * UNROLL4 + j
                    if combine.reached(i, j, 2):
                        sp.wait_ge(sum_ready, n - 1)
                    sp.dma_start(y_in[s].rearrange("p (n k d) -> p n k d", n=PG, k=TOPK),
                                 y_v[:, bass.ds(n * PG, PG), :, :]).then_inc(y_loaded[s], 16)
                if combine.live(i, j, 1):
                    n = i * UNROLL4 + j - 1
                    sp.wait_ge(sum_ready, n + 1)
                    sp.dma_start(out_v[:, bass.ds(n * PG, PG), :],
                                 qx_all[:, bass.ds(n * PG * D, PG * D)].rearrange("p (n d) -> p n d", d=D)).then_inc(stored, 16)

            combine(sp, 1, y_step)
            sp.wait_ge(stored, GROUPS * 16)

        @block.gpsimd
        def _(pool):
            def carry_wait():
                pool.sem_inc(wait_carried, 1)

            for s in range(2):
                pool.memset(rows[s][:, :, :, :], 0.0).then_inc(pads_ready, 1)
            pool.memset(pad_rows[:, :, :], 0.0).then_inc(pads_ready, 1)
            pool.wait_ge(const_loaded, N_CONST)
            pool.wait_ge(pads_ready, 3)
            pool.tensor_copy(pad_rows[:, :, D], const(C_TRASH, 2 * E)).then_inc(pads_ready, 1)
            for s in range(2):
                pool.tensor_copy(blocks(v_blk[s])[:, :, :, HD], parity_mask.unsqueeze(1).to_broadcast([P, HEADS, 2]))
            pool.wait_ge(pads_ready, 4)
            pool.dma_start(sorted_rows[NULL_ROW:NULL_ROW + E * P, :].rearrange("(e p) c -> p e c", p=P), pad_rows[:, E:2 * E, :]).then_inc(padded, 16)
            pool.wait_ge(k_copied, GROUPS)
            pool.wait_ge(q_copied, GROUPS)
            pool.wait_ge(v_copied, GROUPS)

            def expand_step(i, j):
                s = j % 2
                if attend.live(i, j):
                    n = i * UNROLL2 + j
                    if attend.reached(i, j, 2):
                        pool.wait_ge(scores_done, n - 1)
                    k = k_all[:, bass.ds(n * 2 * S, 2 * S)].rearrange("p (t k) -> p t k", t=2)
                    q = qx_all[:, bass.ds(n * 2 * S, 2 * S)].rearrange("p (t k) -> p t k", t=2)
                    pool.tensor_tensor(k_mask[s][:, :, :, :], k.unsqueeze(2).to_broadcast([P, 2, QUAD, S]),
                                       head_mask.unsqueeze(1).unsqueeze(3).to_broadcast([P, 2, QUAD, S]), ALU.mult).then_inc(operands_ready, 1)
                    pool.tensor_tensor(q_blk[s][:, :, :, :], q.unsqueeze(2).to_broadcast([P, 2, 2, S]),
                                       batch_mask.unsqueeze(1).unsqueeze(3).to_broadcast([P, 2, 2, S]), ALU.mult).then_inc(operands_ready, 1)
                if attend.live(i, j, 2):
                    n = i * UNROLL2 + j - 2
                    if attend.reached(i, j, 4):
                        pool.wait_ge(av_done, n - 1)
                    v = v_all[:, bass.ds(n * 2 * D, 2 * D)].rearrange("p (m h d) -> p m h d", h=2, d=HD)
                    pool.tensor_tensor(blocks(v_blk[s])[:, :, :, 0:HD], v,
                                       parity_mask.unsqueeze(1).unsqueeze(3).to_broadcast([P, HEADS, 2, HD]), ALU.mult).then_inc(values_ready, 1)
                if attend.live(i, j, 15):
                    n, g, q = i * UNROLL2 + j - 15, (j - 15) // PG % 2, (j - 15) % PG
                    if q == 0:
                        pool.wait_ge(rows_ready, n + PG)
                        carry_wait()
                    for k in range(TOPK):
                        pool.indirect_dma_start(sorted_rows, bass.IndirectOffsetOnAxis(ap=index[g][:, k, q:q + 1], axis=0),
                                                rows[g][:, q, k, :], None).then_inc(scattered[g], 16)

            attend(pool, 15, expand_step)
            pool.wait_ge(pads_ready, 5)
            for e in range(E):
                pool.indirect_dma_start(sorted_rows, bass.IndirectOffsetOnAxis(ap=pad_index[:, e:e + 1], axis=0),
                                        pad_rows[:, e, :], None).then_inc(padded, 16)

            def send_step(i, j):
                if not experts.live(i, j, 4):
                    return
                t, s = i * UNROLL3 + j - 4, (j - 4) % 4
                pool.wait_ge(y_ready, t + 1)
                carry_wait()
                pool.indirect_dma_start(expert_out, bass.IndirectOffsetOnAxis(ap=y_index[s][:, :], axis=0),
                                        y_out[s], None).then_inc(y_sent[s], 16)

            experts(pool, 4, send_step)

        @block.vector
        def _(dve):
            dve.wait_ge(const_loaded, N_CONST)
            dve.tensor_copy(ident_r[:, :], ident)
            dve.tensor_copy(base[:, :], const(C_REGION, E))
            dve.tensor_copy(dest[:, :, :], const(C_DEST, PG * TOPK).rearrange("p (q k) -> p q k", q=PG))
            dve.wait_ge(bo_done, 1)
            dve.tensor_tensor(bo_sb[:, :], bank[0][0:1, 0:D], bo_sb[:, :], ALU.add)
            dve.wait_ge(tanh_ready, 1)
            dve.tensor_scalar(wo_sb[:, :], wo_sb[:, :], tanh_gate[:, 0:1], None, ALU.mult)
            dve.drain()
            dve.tensor_scalar(bo_sb[:, :], bo_sb[:, :], tanh_gate[0:1, 0:1], None, ALU.mult).then_inc(consts_ready, 1)

            def project_step(i, j):
                s = j % 2
                if project.live(i, j):
                    n, u = i * UNROLL1 + j, i * (UNROLL1 // 2) + j // 2
                    dve.wait_ge(x_loaded[s], (u + 1) * 16)
                    for q in range(PG):
                        dve.bn_stats(stats[:, q, :], x_in[s][:, q * D:q * D + D])
                    dve.drain()
                    for q in range(PG):
                        last = dve.bn_aggr(mv[:, q, :], stats[:, q, :])
                    last.then_inc(var_ready, 1)
                    dve.wait_ge(std_ready, n + 1)
                    dve.reciprocal(rstd[:, :], std[:, :])
                    dve.drain()
                    for q in range(PG):
                        last = dve.tensor_scalar(x_in[s][:, q * D:q * D + D], x_in[s][:, q * D:q * D + D],
                                                 mv[:, q, 0:1], rstd[:, q:q + 1], ALU.subtract, ALU.mult)
                    last.then_inc(xn_ready, 1)
                if project.live(i, j, 1):
                    n = i * UNROLL1 + j - 1
                    dve.wait_ge(v_done, n + 1)
                    for h in range(2):
                        last = dve.tensor_copy(v_all[:, bass.ds(n * 2 * D * PG + h * 512, 512)], bank[6 + h][:, :])
                    last.then_inc(v_copied, 1)

            project(dve, 1, project_step)

            def norm_group(g):
                for q in range(PG):
                    dve.bn_stats(stats[:, q, :], x2g[g][:, q, :])
                dve.drain()
                for q in range(PG):
                    dve.bn_aggr(mv[:, q, :], stats[:, q, :])
                dve.drain()
                dve.tensor_scalar(var[:, :], mv[:, :, 1], EPS, None, ALU.add)
                dve.drain()
                dve.tensor_scalar(newton[:, :].bitcast(U32), var[:, :].bitcast(U32), 1, None, ALU.logical_shift_right)
                dve.drain()
                dve.tensor_scalar(rstd[:, :].bitcast(I32), newton[:, :].bitcast(I32), -1.0, float(MAGIC), ALU.mult, ALU.add)
                dve.drain()
                for _ in range(3):
                    dve.tensor_tensor(newton[:, :], rstd[:, :], rstd[:, :], ALU.mult)
                    dve.drain()
                    dve.scalar_tensor_tensor(newton[:, :], newton[:, :], -0.5, var[:, :], ALU.mult, ALU.mult)
                    dve.drain()
                    dve.scalar_tensor_tensor(rstd[:, :], newton[:, :], 1.5, rstd[:, :], ALU.add, ALU.mult)
                    dve.drain()
                for q in range(PG):
                    last = dve.tensor_scalar(x2g[g][:, q, :], x2g[g][:, q, :], mv[:, q, 0:1], rstd[:, q:q + 1], ALU.subtract, ALU.mult)
                last.then_inc(xn2_ready, 1)

            def choose(g):
                rank = const(C_RANK, E).unsqueeze(1).to_broadcast([P, PG, E])
                spread = lambda v: v[:, :].unsqueeze(2).to_broadcast([P, PG, E])
                left = logits[g][:, :, :]
                for k, top in ((0, best), (1, second)):
                    dve.tensor_reduce(top[:, :], left, AX.X, ALU.max)
                    dve.drain()
                    dve.tensor_tensor(work[:, 0], left, spread(top), ALU.is_equal)
                    dve.drain()
                    dve.tensor_tensor(work[:, 0], work[:, 0], rank, ALU.mult)
                    dve.drain()
                    dve.tensor_reduce(picked[:, :], work[:, 0], AX.X, ALU.max)
                    dve.drain()
                    dve.tensor_tensor(chosen[:, k], rank, spread(picked), ALU.is_equal)
                    dve.drain()
                    if k == 0:
                        dve.scalar_tensor_tensor(rest[:, :, :], chosen[:, 0], BELOW_ALL, left, ALU.mult, ALU.add)
                        dve.drain()
                        left = rest[:, :, :]
                dve.tensor_tensor(either[:, :, :], chosen[:, 0], chosen[:, 1], ALU.add)
                dve.tensor_tensor(gap[:, :], second[:, :], best[:, :], ALU.subtract).then_inc(gap_ready, 1)

            def place_group(i, j, g):
                dve.tensor_tensor(place[:, :, :], aux[:, AUX_R:AUX_R + PG * E].rearrange("p (q e) -> p q e", e=E),
                                  base[:, :].unsqueeze(1).to_broadcast([P, PG, E]), ALU.add)
                dve.drain()
                dve.tensor_tensor(base[:, :], aux[:, AUX_T:AUX_T + E], base[:, :], ALU.add).then_inc(mid_read, 1)
                for k in range(TOPK):
                    dve.tensor_tensor(work[:, k], chosen[:, k], place[:, :, :], ALU.mult)
                dve.drain()
                dve.tensor_reduce(place_of[:, :, :], work[:, :, :, :], AX.X, ALU.add)
                dve.drain()
                if attend.reached(i, j, 14 + 2 * PG):
                    use = i * (UNROLL2 // (2 * PG)) + (j - 14) // (2 * PG)
                    dve.wait_ge(scattered[g], use * PG * TOPK * 16)
                dve.tensor_copy(index[g][:, :, :], place_of[:, :, :])
                dve.wait_ge(rows_copied, (i * UNROLL2 + j - 14) // PG + 1 if isinstance(i, int) else i * (UNROLL2 // PG) + (j - 14) // PG + 1)
                dve.tensor_copy(rows[g][:, :, :, D], dest[:, :, :])
                dve.drain()
                dve.tensor_scalar(dest[:, :, :], dest[:, :, :], float(PG * P * TOPK), None, ALU.add)
                dve.wait_ge(ratio_ready, (i * UNROLL2 + j - 14) // PG + 1 if isinstance(i, int) else i * (UNROLL2 // PG) + (j - 14) // PG + 1)
                dve.tensor_scalar(share[:, :], ratio[:, :], 1.0, None, ALU.add)
                dve.drain()
                dve.reciprocal(share[:, :], share[:, :])
                dve.drain()
                dve.tensor_scalar(share[:, :], share[:, :], tanh_gate[:, 1:2], None, ALU.mult)
                dve.drain()
                dve.tensor_copy(rows[g][:, :, 0, D + 1], share[:, :])
                dve.tensor_tensor(rows[g][:, :, 1, D + 1], share[:, :], ratio[:, :], ALU.mult).then_inc(rows_ready, PG)

            def attend_step(i, j):
                m = i * UNROLL2 + j
                if attend.live(i, j):
                    s = j % 2
                    dve.wait_ge(scores_done, m + 1)
                    if attend.reached(i, j, 2):
                        dve.wait_ge(shifted, m - 1)
                    for half in range(2):
                        last = dve.tensor_reduce(neg_max[s][:, half * 8:half * 8 + 8],
                                                 scores[s][half][:, :].rearrange("p (h k) -> p h k", k=S), AX.X, ALU.max, negate=True)
                    last.then_inc(max_ready, 1)
                x2_live, turn_live = attend.live(i, j, 5), attend.live(i, j, 9)
                place_live = (j - 14) % PG == 0 and attend.live(i, j, 14)
                if x2_live or turn_live or place_live:
                    dve.wait_ge(mid_done, m - 4 if not isinstance(m, int) or m < ATTN_LAST else ATTN_LAST - 4)
                if turn_live:
                    s = (j - 9) % 2
                    last = dve.tensor_copy(xn2_t[s][:, :], aux[:, AUX_X:AUX_X + D])
                    if not x2_live and not place_live:
                        last.then_inc(mid_read, 1)
                if x2_live:
                    n, s, g, q = m - 5, (j - 5) % 2, (j - 5) // PG % 2, (j - 5) % PG
                    use = i * (UNROLL2 // 2) + (j - 5) // 2
                    dve.wait_ge(res_loaded[s], (use + 1) * 16)
                    if q == 0 and attend.reached(i, j, 5 + 2 * PG):
                        dve.wait_ge(rows_copied, n // PG - 1 if isinstance(n, int) else i * (UNROLL2 // PG) + (j - 5) // PG - 1)
                    last = dve.tensor_tensor(x2g[g][:, q, :], aux[:, AUX_O:AUX_O + D], x_res[s][:, :], ALU.add)
                    if not place_live:
                        last.then_inc(mid_read, 1)
                    dve.drain()
                    dve.tensor_copy(qx_all[:, bass.ds(n * D, D)], x2g[g][:, q, :]).then_inc(x2_ready, 1)
                if place_live:
                    place_group(i, j, (j - 14) // PG % 2)
                if attend.live(i, j, 2):
                    n, s = m - 2, j % 2
                    dve.wait_ge(t_done[1], n + 1)
                    if attend.reached(i, j, 4):
                        dve.wait_ge(av_done, n - 1)
                    dve.tensor_copy(probs_t[s][:, 512:1024], bank[5][:, :]).then_inc(t_copied[1], 1)
                if attend.live(i, j, 3):
                    n, s = m - 3, (j - 3) % 2
                    dve.wait_ge(av_done, n + 1)
                    if attend.reached(i, j, 5):
                        dve.wait_ge(end_done, n - 1)
                    halves = [(slice(64 * b, 64 * b + 64), bank[6][64 * b:64 * b + 64, 0:HEADS // 2 * VB].rearrange(
                        "p (j b h e) -> p j b h e", b=2, h=2, e=HD + 1)[:, :, b]) for b in range(2)]
                    for rows_, o in halves:
                        dve.reciprocal(rsum[rows_, :].rearrange("p (j h) -> p j h", h=2), o[:, :, :, HD])
                    dve.drain()
                    for rows_, o in halves:
                        r = rsum[rows_, :].rearrange("p (j h) -> p j h", h=2).unsqueeze(3).to_broadcast([64, HEADS // 2, 2, HD])
                        last = dve.tensor_tensor(o_buf[s][rows_, :].rearrange("p (j h d) -> p j h d", h=2, d=HD),
                                                 o[:, :, :, 0:HD], r, ALU.mult)
                    last.then_inc(o_ready, 1)
                if (j - 8) % PG == 0 and attend.live(i, j, 8):
                    norm_group((j - 8) // PG % 2)
                if (j - 13) % PG == 0 and attend.live(i, j, 13):
                    dve.wait_ge(end_read, m - 4 if not isinstance(m, int) or m < ATTN_LAST else ATTN_LAST - 4)
                    choose((j - 13) // PG % 2)

            attend(dve, 15, attend_step)

            dve.tensor_tensor(pad_place[:, :], base[:, :], const(C_PART).to_broadcast([P, E]), ALU.add)
            dve.tensor_tensor(count[:, :], base[:, :], const(C_REGION, E), ALU.subtract)
            dve.drain()
            dve.tensor_copy(pad_index[:, :], pad_place[:, :]).then_inc(pads_ready, 1)
            dve.tensor_scalar(count[:, :], count[:, :], float(P - 1), None, ALU.add)
            dve.drain()
            dve.tensor_copy(count_i[:, :], count[:, :])
            dve.drain()
            dve.tensor_scalar(count_i[:, :], count_i[:, :], 7, None, ALU.logical_shift_right)
            dve.drain()
            dve.tensor_copy(tiles_of[:, :], count_i[:, :])
            dve.drain()
            dve.tensor_scalar(skip[:, :], tiles_of[:, :], -float(P), float(REGION), ALU.mult, ALU.add)
            src = tiles_of
            for n, step in enumerate((1, 2, 4)):
                dst = upto[n % 2]
                dve.tensor_copy(dst[:, 0:step], src[:, 0:step])
                dve.tensor_tensor(dst[:, step:E], src[:, step:E], src[:, 0:E - step], ALU.add)
                dve.drain()
                src = dst
            tile = const_sb[0:1, C_TILE:C_TILE + TILES]
            dve.tensor_tensor(passed, tile.unsqueeze(2).to_broadcast([1, TILES, E]),
                              src[0:1, :].unsqueeze(1).to_broadcast([1, TILES, E]), ALU.is_ge)
            dve.drain()
            dve.tensor_tensor(skipped, passed, skip[0:1, :].unsqueeze(1).to_broadcast([1, TILES, E]), ALU.mult)
            dve.tensor_reduce(tile_f[:, 0, :], passed, AX.X, ALU.add)
            dve.drain()
            dve.tensor_reduce(tile_f[:, 1, :], skipped, AX.X, ALU.add)
            dve.tensor_scalar(tile_expert[:, :], tile_f[:, 0, :], float(E - 1), None, ALU.min)
            dve.drain()
            dve.scalar_tensor_tensor(tile_f[:, 1, :], tile, float(P), tile_f[:, 1, :], ALU.mult, ALU.add)
            dve.drain()
            dve.tensor_copy(tile_row[:, :], tile_f[:, 1, :]).then_inc(table_ready, 1)
            for s in range(2):
                dve.memset(hidden[s][:, H:HP], 0.0)

            def expert_step(i, j):
                t = i * UNROLL3 + j
                if experts.live(i, j, 1):
                    s, s4 = (j - 1) % 2, (j - 1) % 4
                    dve.wait_ge(gated_ready, t)
                    if experts.reached(i, j, 3):
                        dve.wait_ge(hidden_turned, t - 2)
                    dve.scalar_tensor_tensor(hidden[s][:, 0:H], gated[s], row_in[s4][:, D + 1:D + 2], bank[3 + s][:, 0:H],
                                             ALU.mult, ALU.mult)
                    if experts.reached(i, j, 5):
                        use = i * (UNROLL3 // 4) + (j - 1) // 4
                        dve.wait_ge(y_sent[s4], use * 16)
                    dve.tensor_copy(y_index[s4][:, :], row_in[s4][:, D:D + 1]).then_inc(hidden_ready, 1)
                if experts.live(i, j, 3):
                    s, s4 = (j - 3) % 2, (j - 3) % 4
                    dve.wait_ge(down_done, t - 2)
                    dve.tensor_copy(y_out[s4], bank[6 + s][:, 0:D]).then_inc(y_ready, 1)

            experts(dve, 3, expert_step)

            def sum_step(i, j):
                s, n, u = j % 2, i * UNROLL4 + j, i * (UNROLL4 // 2) + j // 2
                dve.wait_ge(y_loaded[s], (u + 1) * 16)
                y = y_in[s].rearrange("p (n k d) -> p n k d", n=PG, k=TOPK)
                x2 = qx_all[:, bass.ds(n * PG * D, PG * D)].rearrange("p (n d) -> p n d", d=D)
                dve.tensor_tensor(y[:, :, 0, :], y[:, :, 0, :], y[:, :, 1, :], ALU.add)
                dve.drain()
                dve.tensor_tensor(x2, x2, y[:, :, 0, :], ALU.add).then_inc(sum_ready, 1)

            combine(dve, 0, sum_step)

        @block.scalar
        def _(act):
            act.wait_ge(const_loaded, N_CONST)
            act.activation(tanh_gate[:, :], gate_sb[:, :], ACT.Tanh).then_inc(tanh_ready, 1)

            def project_step(i, j):
                s = j % 2
                n = i * UNROLL1 + j
                if project.live(i, j):
                    act.wait_ge(var_ready, n + 1)
                    act.activation(std[:, :], mv[:, :, 1], ACT.Sqrt, bias=const(C_EPS)).then_inc(std_ready, 1)
                    act.wait_ge(ct_done, n + 1)
                    if project.reached(i, j, 2):
                        act.wait_ge(v_done, n - 1)
                    act.copy(c_t[s], bank[2 + s][:, :]).then_inc(ct_copied, 1)
                    act.wait_ge(xt_done, n + 1)
                    act.copy(xn_t[s], bank[s][:, :]).then_inc(xt_copied, 1)
                if project.live(i, j, 1):
                    n = n - 1
                    for store, out_bank, bias, done, copied in ((k_all, bank[4], 2, k_done, k_copied), (qx_all, bank[5], 0, q_done, q_copied)):
                        act.wait_ge(done, n + 1)
                        for t in range(2):
                            dst = store[:, bass.ds(n * 2 * S * PG, 2 * S * PG)].rearrange("p (q t k) -> p q t k", q=PG, t=2)
                            last = act.activation(dst[:, :, t, :], out_bank[:, 256 * t:256 * t + 256].rearrange("p (q k) -> p q k", q=PG),
                                                  ACT.Identity, bias=bias_sb[:, bias + t:bias + t + 1])
                        last.then_inc(copied, 1)

            project(act, 1, project_step)

            def attend_step(i, j):
                m = i * UNROLL2 + j
                if (j - 12) % PG == 0 and attend.live(i, j, 12):
                    g = (j - 12) // PG % 2
                    count_ = (m - 12) // PG if isinstance(i, int) else i * (UNROLL2 // PG) + (j - 12) // PG
                    if attend.reached(i, j, 12 + 2 * PG):
                        use = i * (UNROLL2 // (2 * PG)) + (j - 12) // (2 * PG)
                        act.wait_ge(scattered[g], use * PG * TOPK * 16)
                    act.wait_ge(xn2_ready, count_ + 1)
                    act.copy(rows[g][:, :, :, 0:D], x2g[g][:, :, :].unsqueeze(2).to_broadcast([P, PG, TOPK, D])).then_inc(rows_copied, 1)
                if attend.live(i, j, 1):
                    n, s = m - 1, (j - 1) % 2
                    act.wait_ge(shifted, n + 1)
                    if attend.reached(i, j, 3):
                        act.wait_ge(t_done[1], n - 1)
                    for half in range(2):
                        last = act.activation(probs[s][:, half * 512:half * 512 + 512], scores[s][half][:, :], ACT.Exp, scale=HD ** -0.5)
                    last.then_inc(probs_ready, 1)
                if attend.live(i, j, 2):
                    n, s = m - 2, j % 2
                    act.wait_ge(t_done[0], n + 1)
                    if attend.reached(i, j, 4):
                        act.wait_ge(av_done, n - 1)
                    act.copy(probs_t[s][:, 0:512], bank[4][:, :]).then_inc(t_copied[0], 1)
                if attend.live(i, j, 4) or attend.live(i, j, 9):
                    act.wait_ge(end_done, m - 3)
                    if attend.live(i, j, 9):
                        g, q = (j - 9) // PG % 2, (j - 9) % PG
                        last = act.copy(logits[g][:, q, :], aux[:, AUX_L:AUX_L + E])
                    if attend.live(i, j, 4):
                        if attend.reached(i, j, 6):
                            act.wait_ge(mid_done, m - 5)
                        last = act.copy(o_t[(j - 4) % 2][:, :], aux[:, AUX_O:AUX_O + D])
                    last.then_inc(end_read, 1)
                if (j - 14) % PG == 0 and attend.live(i, j, 14):
                    count_ = (m - 14) // PG if isinstance(i, int) else i * (UNROLL2 // PG) + (j - 14) // PG
                    act.wait_ge(gap_ready, count_ + 1)
                    act.activation(ratio[:, :], gap[:, :], ACT.Exp).then_inc(ratio_ready, 1)

            attend(act, 15, attend_step)

            def expert_step(i, j):
                t = i * UNROLL3 + j
                if experts.live(i, j):
                    s = j % 2
                    act.wait_ge(row_turned, t + 1)
                    if experts.reached(i, j, 2):
                        act.wait_ge(up_done, t - 1)
                    act.copy(xt[s], bank[0][:, 0:D]).then_inc(row_copied, 1)
                if experts.live(i, j, 1):
                    s = (j - 1) % 2
                    act.wait_ge(up_done, t)
                    if experts.reached(i, j, 3):
                        act.wait_ge(hidden_ready, t - 2)
                    act.activation(gated[s], bank[1 + s][:, 0:H], ACT.Silu).then_inc(gated_ready, 1)
                if experts.live(i, j, 2):
                    s = j % 2
                    act.wait_ge(hidden_turned, t - 1)
                    if experts.reached(i, j, 4):
                        act.wait_ge(down_done, t - 3)
                    act.copy(hidden_t[s], bank[5][:, 0:HP]).then_inc(hidden_copied, 1)

            experts(act, 2, expert_step)

        @block.tensor
        def _(pe):
            pe.wait_ge(const_loaded, N_CONST)
            pe.matmul(bank[0][0:1, 0:D], bv_sb[:, :], wo_sb[:, :], start=True, stop=True).then_inc(bo_done, 1)
            pe.wait_ge(consts_ready, 1)

            def project_step(i, j):
                s = j % 2
                if project.live(i, j):
                    n, u = i * UNROLL1 + j, i * (UNROLL1 // 2) + j // 2
                    pe.wait_ge(c_loaded[s], (u + 1) * 16)
                    if project.reached(i, j, 2):
                        pe.wait_ge(ct_copied, n - 1)
                    for q in range(PG):
                        last = pe.transpose(bank[2 + s][:, q * D:q * D + D], c_in[s][:, q * D:q * D + D], ident)
                    last.then_inc(ct_done, 1)
                    pe.wait_ge(xn_ready, n + 1)
                    if project.reached(i, j, 2):
                        pe.wait_ge(xt_copied, n - 1)
                    for q in range(PG):
                        last = pe.transpose(bank[s][:, q * D:q * D + D], x_in[s][:, q * D:q * D + D], ident)
                    last.then_inc(xt_done, 1)
                if project.live(i, j, 1):
                    n, s = i * UNROLL1 + j - 1, (j - 1) % 2
                    for src, w0, out_bank, ready, free, done in ((c_t[s], D, bank[4], ct_copied, k_copied, k_done),
                                                                 (xn_t[s], 0, bank[5], xt_copied, q_copied, q_done)):
                        pe.wait_ge(ready, n + 1)
                        if project.reached(i, j, 2):
                            pe.wait_ge(free, n)
                        rhs = src.rearrange("p (q b k) -> p b q k", q=PG, b=2)
                        for t in range(2):
                            for half in range(2):
                                for b in range(2):
                                    c = 64 * half + 32 * b
                                    f = w0 + 64 * half + 32 * t
                                    last = pe.matmul(out_bank[c:c + 32, 256 * t:256 * t + 256], wqkv_sb[:, f:f + 32], rhs[:, b],
                                                     start=True, stop=True)
                        last.then_inc(done, 1)
                    if project.reached(i, j, 2):
                        pe.wait_ge(v_copied, n)
                    for q in range(PG):
                        for b in range(2):
                            for h in range(2):
                                last = pe.matmul(bank[6 + q // 2][64 * h:64 * h + 64, (q % 2 * 2 + b) * D:(q % 2 * 2 + b + 1) * D],
                                                 c_t[s][:, (2 * q + b) * S:(2 * q + b + 1) * S], wqkv_sb[:, 2 * D:3 * D],
                                                 start=True, stop=True)
                    last.then_inc(v_done, 1)

            project(pe, 1, project_step)
            pe.wait_ge(k_copied, GROUPS)
            pe.wait_ge(q_copied, GROUPS)
            pe.wait_ge(v_copied, GROUPS)

            def attend_step(i, j):
                m = i * UNROLL2 + j
                if attend.live(i, j):
                    s = j % 2
                    pe.wait_ge(operands_ready, 2 * m + 2)
                    if attend.reached(i, j, 2):
                        pe.wait_ge(probs_ready, m - 1)
                    for t in range(2):
                        for half in range(2):
                            last = pe.matmul(scores[s][half][:, 256 * t:256 * t + 256],
                                             q_blk[s][64 * half:64 * half + 64, t, :, :],
                                             k_mask[s][64 * half:64 * half + 64, t, :, :],
                                             start=t == 0, stop=t == 1, skip_group_check=True)
                    last.then_inc(scores_done, 1)
                x2_live, turn_live = attend.live(i, j, 5), attend.live(i, j, 9)
                place_live = (j - 14) % PG == 0 and attend.live(i, j, 14)
                if x2_live or turn_live or place_live:
                    pe.wait_ge(end_read, m - 4 if not isinstance(m, int) or m < ATTN_LAST else ATTN_LAST - 4)
                    if turn_live:
                        g, q = (j - 9) // PG % 2, (j - 9) % PG
                        count_ = (m - 9) // PG if isinstance(i, int) else i * (UNROLL2 // PG) + (j - 9) // PG
                        if q == 0:
                            pe.wait_ge(xn2_ready, count_ + 1)
                        last = pe.transpose(aux[:, AUX_X:AUX_X + D], x2g[g][:, q, :], ident)
                    if x2_live:
                        s = (j - 5) % 2
                        pe.matmul(aux[:, AUX_O:AUX_O + D], o_t[s][:, :], wo_sb[:, :], start=True, stop=False)
                        last = pe.matmul(aux[:, AUX_O:AUX_O + D], ones[0:1, :], bo_sb[0:1, :], start=False, stop=True)
                    if place_live:
                        count_ = (m - 14) // PG if isinstance(i, int) else i * (UNROLL2 // PG) + (j - 14) // PG
                        pe.wait_ge(gap_ready, count_ + 1)
                        pe.matmul(aux[:, AUX_R:AUX_R + PG * E], tri, either[:, :, :], start=True, stop=False, skip_group_check=True)
                        for q in range(PG - 1):
                            pe.matmul(aux[:, AUX_R + (q + 1) * E:AUX_R + PG * E], ones,
                                      either[:, q:q + 1, :].to_broadcast([P, PG - 1 - q, E]), start=False, stop=q == PG - 2,
                                      skip_group_check=True)
                        for q in range(PG):
                            last = pe.matmul(aux[:, AUX_T:AUX_T + E], ones, either[:, q, :], start=q == 0, stop=q == PG - 1,
                                             skip_group_check=True)
                    last.then_inc(mid_done, 1)
                if attend.live(i, j, 1):
                    n, s = m - 1, (j - 1) % 2
                    pe.wait_ge(max_ready, n + 1)
                    for half in range(2):
                        last = pe.matmul(scores[s][half][:, :], ident_r[:, :],
                                         neg_max[s][:, half * 8:half * 8 + 8].unsqueeze(2).to_broadcast([P, 8, S]),
                                         start=False, stop=True, skip_group_check=True)
                    last.then_inc(shifted, 1)
                if attend.live(i, j, 2):
                    n, s = m - 2, (j - 2) % 2
                    pe.wait_ge(probs_ready, n + 1)
                    for half in range(2):
                        if attend.reached(i, j, 3):
                            pe.wait_ge(t_copied[half], n)
                        for c in range(4):
                            last = pe.transpose(bank[4 + half][:, c * P:c * P + P], probs[s][:, half * 512 + c * P:half * 512 + c * P + P], ident)
                        last.then_inc(t_done[half], 1)
                if attend.live(i, j, 3):
                    n, s = m - 3, (j - 3) % 2
                    pe.wait_ge(values_ready, n + 1)
                    if attend.reached(i, j, 4):
                        pe.wait_ge(o_ready, n)
                    v_pair = v_blk[s][:, :].rearrange("p (b j c) -> p b j c", b=2, j=HEADS // 2)
                    for half in range(2):
                        pe.wait_ge(t_copied[half], n + 1)
                        for c in range(4):
                            p = half * 4 + c
                            last = pe.matmul(bank[6][:, p * VB:p * VB + VB], probs_t[s][:, p * P:p * P + P],
                                             v_pair[:, :, p], start=True, stop=True)
                    last.then_inc(av_done, 1)
                if attend.live(i, j, 4) or attend.live(i, j, 9):
                    if attend.reached(i, j, 5):
                        pe.wait_ge(mid_read, m - 4)
                    if attend.live(i, j, 9):
                        last = pe.matmul(aux[:, AUX_L:AUX_L + E], xn2_t[(j - 9) % 2][:, :], wgate_sb[:, :], start=True, stop=True)
                    if attend.live(i, j, 4):
                        pe.wait_ge(o_ready, m - 3)
                        last = pe.transpose(aux[:, AUX_O:AUX_O + D], o_buf[j % 2][:, :], ident)
                    last.then_inc(end_done, 1)

            attend(pe, 15, attend_step)
            pe.wait_ge(table_ready, 1)
            pe.wait_ge(w13_loaded, 16)

            def expert_step(i, j):
                t = i * UNROLL3 + j
                if experts.live(i, j):
                    u = i * (UNROLL3 // 4) + j // 4
                    pe.wait_ge(row_loaded[j % 4], (u + 1) * 16)
                    if experts.reached(i, j, 1):
                        pe.wait_ge(row_copied, t)
                    pe.transpose(bank[0][:, 0:D], row_in[j % 4][:, 0:D], ident).then_inc(row_turned, 1)
                if experts.live(i, j, 1):
                    s = (j - 1) % 2
                    e = pe.value_load(tile_expert[0:1, bass.ds(t - 1, 1)], min_val=0, max_val=E - 1)
                    pe.wait_ge(row_copied, t)
                    if experts.reached(i, j, 3):
                        pe.wait_ge(hidden_ready, t - 2)
                    for k in range(2):
                        last = pe.matmul(bank[1 + 2 * k + s][:, 0:H], xt[s], w13_sb[:, bass.ds(e * (2 * H) + k * H, H)], start=True, stop=True)
                    last.then_inc(up_done, 1)
                if experts.live(i, j, 2):
                    s = j % 2
                    pe.wait_ge(hidden_ready, t - 1)
                    if experts.reached(i, j, 3):
                        pe.wait_ge(hidden_copied, t - 2)
                    for c in range(CHUNKS):
                        last = pe.transpose(bank[5][:, c * P:c * P + P], hidden[s][:, c * P:c * P + P], ident)
                    last.then_inc(hidden_turned, 1)
                if experts.live(i, j, 3):
                    s = (j - 3) % 2
                    e = pe.value_load(tile_expert[0:1, bass.ds(t - 3, 1)], min_val=0, max_val=E - 1)
                    pe.wait_ge(hidden_copied, t - 2)
                    if experts.reached(i, j, 5):
                        pe.wait_ge(y_ready, t - 4)
                    for c in range(CHUNKS):
                        last = pe.matmul(bank[6 + s][:, 0:D], hidden_t[s][:, c * P:c * P + P],
                                         w2_sb[:, bass.ds(e * D + c * E * D, D)], start=c == 0, stop=c == CHUNKS - 1)
                    last.then_inc(down_done, 1)

            experts(pe, 3, expert_step)


def constants():
    import numpy as np
    p = np.arange(P)
    columns = [np.eye(P), np.triu(np.ones((P, P)), 1), np.ones((P, P)),
               (p // HD % QUAD)[:, None] == np.arange(QUAD)[None],
               (p // 32 % 2)[:, None] == np.arange(2)[None],
               (p // S)[:, None] == np.arange(2)[None],
               np.full((P, 1), EPS),
               np.tile(E - np.arange(E), (P, 1)),
               np.tile(REGION * np.arange(E), (P, 1)),
               TOPK * (P * (np.arange(PG * TOPK) // TOPK)[None] + p[:, None]) + (np.arange(PG * TOPK) % TOPK)[None],
               p[:, None], TRASH + P * np.arange(2 * E)[None] + p[:, None],
               np.tile(np.arange(TILES), (P, 1))]
    return np.concatenate([np.asarray(c, np.float32) for c in columns], axis=1)


def kernel(**inputs):
    import numpy as np
    import concourse.bacc as bacc
    from concourse import mybir
    from concourse.bass_utils import run_bass_kernel_spmd

    p = np.arange(P)
    feature = [64 * (p // 64) + 32 * t + p % 32 for t in range(2)]
    bq, bkv = inputs["L0_xattn_bq"], inputs["L0_xattn_bkv"]
    w1, w3, w2 = inputs["L0_ffn_w1"], inputs["L0_ffn_w3"], inputs["L0_ffn_w2"]
    w13 = np.concatenate([w1.transpose(2, 0, 1), w3.transpose(2, 0, 1)], axis=2).reshape(D, E * 2 * H)
    w2p = np.pad(w2.transpose(2, 0, 1), ((0, HP - H), (0, 0), (0, 0)))
    w2p = w2p.reshape(CHUNKS, P, E * D).transpose(1, 0, 2).reshape(P, CHUNKS * E * D)
    arrays = {
        "x": inputs["x"],
        "ctx": inputs["ctx_1024"],
        "consts": constants(),
        "qk_bias": np.stack([bq[feature[0]], bq[feature[1]], bkv[:D][feature[0]], bkv[:D][feature[1]]], axis=1),
        "gates": np.concatenate([np.broadcast_to(inputs["g_xattn"], (P, 1)), np.broadcast_to(inputs["g_ffn"], (P, 1))], axis=1),
        "bv": bkv[D:].reshape(P, 1),
        "bo": inputs["L0_xattn_bo"].reshape(1, D),
        "w_qkv": np.concatenate([inputs["L0_xattn_Wq"], inputs["L0_xattn_Wkv"]], axis=1),
        "w_o": inputs["L0_xattn_Wo"],
        "w_gate": inputs["L0_ffn_gate_w"].T,
        "w13": w13,
        "w2": w2p,
    }
    arrays = {n: np.ascontiguousarray(a) for n, a in arrays.items()}
    nc = bacc.Bacc("TRN2", target_bir_lowering=False, num_devices=1)
    args = [nc.dram_tensor("in_" + n, a.shape, mybir.dt.from_np(a.dtype), kind="ExternalInput").ap() for n, a in arrays.items()]
    out = nc.dram_tensor("out", (B, S, D), mybir.dt.from_np(np.dtype("float32")), kind="ExternalOutput").ap()
    build(nc, *args, out)
    r = run_bass_kernel_spmd(nc, [{"in_" + n: a for n, a in arrays.items()}], core_ids=[0])
    return r.results[0]["out"]
```

```python
from contextlib import ExitStack

import concourse.bass as bass
from concourse import mybir

FP32 = mybir.dt.float32
FP32R = mybir.dt.float32r
U32 = mybir.dt.uint32
I32 = mybir.dt.int32
ALU = mybir.AluOpType
ACT = mybir.ActivationFunctionType
AX = mybir.AxisListType

B, S, D = 128, 64, 128
HEADS = 16
HD = D // HEADS
P = 128
TOKENS = B * S
PAIRS = TOKENS // P
PG = 4
GROUPS = PAIRS // PG
QUAD = 4
EPS = 1e-5
UNROLL1, UNROLL2, UNROLL3, UNROLL4 = 4, 8, 8, 4
AT_X2, AT_NORM, AT_TURN, AT_CHOOSE, AT_COPY, AT_PLACE, AT_SEND = 5, 8, 11, 15, 17, 18, 20
VB = 2 * 2 * (HD + 1)

E, H, TOPK = 8, 352, 2
CHUNKS = 3
HP = CHUNKS * P
REGION = TOKENS + P
NULL_ROW = E * REGION
ROW = D + 4
TRASH = TOPK * TOKENS
TILES = TOPK * TOKENS // P + E
BELOW_ALL = -3e38
MAGIC = 0x5F3759DF

C_IDENT, C_TRI, C_ONES = 0, P, 2 * P
C_HEAD = 3 * P
C_BATCH = C_HEAD + QUAD
C_PARITY = C_BATCH + 2
C_EPS = C_PARITY + 2
C_RANK = C_EPS + 1
C_REGION = C_RANK + E
C_DEST = C_REGION + E
C_TRASH = C_DEST + PG * TOPK
C_TILE = C_TRASH + 2 * E
C_END = C_TILE + TILES


def build(nc, x, ctx, consts, qk_bias, gates, bv, bo, w_qkv, w_o, w_gate, w13, w2, out):
    es = ExitStack()
    with es:
        sb = lambda name, shape, dt=FP32: es.enter_context(nc.sbuf_tensor(name, shape, dt))
        sem = lambda name: es.enter_context(nc.semaphore(name))
        pair_of = lambda make: [make(0), make(1)]

        const_sb = sb("const_sb", [P, C_END])
        const = lambda at, n=1: const_sb[:, at:at + n]
        ident, tri, ones = const(C_IDENT, P), const(C_TRI, P), const(C_ONES, P)
        head_mask = const(C_HEAD, QUAD)
        batch_mask = const(C_BATCH, 2)
        parity_mask = const(C_PARITY, 2)
        ident_r = sb("ident_r", [P, P], FP32R)
        tri_r = sb("tri_r", [P, P], FP32R)
        ones_r = sb("ones_r", [P, P], FP32R)
        bias_sb = sb("bias_sb", [P, 4])
        gate_sb = sb("gate_sb", [P, 2])
        tanh_gate = sb("tanh_gate", [P, 2])
        bv_sb = sb("bv_sb", [P, 1])
        bo_sb = sb("bo_sb", [1, D])
        wqkv_sb = sb("wqkv_sb", [P, 3 * D])
        wo_sb = sb("wo_sb", [P, D])
        wgate_sb = sb("wgate_sb", [P, E])
        w2_sb = sb("w2_sb", [P, CHUNKS * E * D])

        k_all = sb("k_all", [P, PAIRS * 2 * S])
        qx_all = sb("qx_all", [P, PAIRS * 2 * S])
        v_all = sb("v_all", [P, PAIRS * 2 * D])
        w13_sb = k_all[:, 0:E * 2 * H]

        arena = sb("arena", [P, 5120])
        x_in = [arena[:, 512 * s:512 * s + 512] for s in range(4)]
        c_t = [arena[:, 2048 + 512 * s:2560 + 512 * s] for s in range(4)]
        xn_t = pair_of(lambda s: arena[:, 4096 + 512 * s:4608 + 512 * s])
        probs = pair_of(lambda s: arena[:, 1024 * s:1024 * s + 1024])
        probs_t = pair_of(lambda s: arena[:, 2048 + 1024 * s:3072 + 1024 * s])
        k_mask = pair_of(lambda s: sb(f"k_mask{s}", [P, 2, QUAD, S]))
        q_blk = pair_of(lambda s: sb(f"q_blk{s}", [P, 2, 2, S]))
        v_blk = pair_of(lambda s: sb(f"v_blk{s}", [P, HEADS // 2 * VB]))
        neg_max = pair_of(lambda s: sb(f"neg_max{s}", [P, HEADS], FP32R))
        rsum = sb("rsum", [P, HEADS])
        o_buf = pair_of(lambda s: sb(f"o_buf{s}", [P, D]))
        o_t = pair_of(lambda s: sb(f"o_t{s}", [P, D]))
        x_res = pair_of(lambda s: sb(f"x_res{s}", [P, D]))
        stats = sb("stats", [P, PG, 6])
        mv = sb("mv", [P, PG, 2])
        std = sb("std", [P, PG])
        rstd = sb("rstd", [P, PG])
        var = sb("var", [P, PG])
        newton = sb("newton", [P, PG])
        x2g = pair_of(lambda s: sb(f"x2g{s}", [P, PG, D]))
        xn2g = pair_of(lambda s: sb(f"xn2g{s}", [P, PG, D]))
        xn2_t = pair_of(lambda s: sb(f"xn2_t{s}", [P, D]))
        logits = pair_of(lambda s: sb(f"logits{s}", [P, PG, E]))
        best = sb("best", [P, PG])
        second = sb("second", [P, PG])
        picked = sb("picked", [P, PG])
        rest = sb("rest", [P, PG, E])
        work = sb("work", [P, TOPK, PG, E])
        chosen = sb("chosen", [P, TOPK, PG, E])
        either = sb("either", [P, PG + 1, E], FP32R)
        gap = sb("gap", [P, PG])
        ratio = sb("ratio", [P, PG])
        share = sb("share", [P, PG])
        place = sb("place", [P, PG, E])
        place_of = sb("place_of", [P, TOPK, PG])
        index = pair_of(lambda s: sb(f"index{s}", [P, TOPK, PG], U32))
        base = sb("base", [P, E])
        dest = sb("dest", [P, PG, TOPK])
        rows = pair_of(lambda s: sb(f"rows{s}", [P, PG, TOPK, ROW]))
        pad_rows = sb("pad_rows", [P, 2 * E, ROW])
        first_pad = sb("first_pad", [P, E], I32)

        count = sb("count", [P, E])
        count_i = sb("count_i", [P, E], I32)
        tiles_of = sb("tiles_of", [P, E])
        upto = pair_of(lambda s: sb(f"upto{s}", [P, E]))
        skip = sb("skip", [P, E])
        passed = v_all[0:1, 0:TILES * E].rearrange("p (t e) -> p t e", e=E)
        skipped = v_all[0:1, TILES * E:2 * TILES * E].rearrange("p (t e) -> p t e", e=E)
        tile_f = arena[0:1, 4096:4096 + 2 * TILES].rearrange("p (k t) -> p k t", k=2)
        tile_row = sb("tile_row", [1, TILES], I32)
        tile_up = sb("tile_up", [1, TILES], I32)
        tile_down = sb("tile_down", [1, TILES], I32)

        at3 = [2 * TILES * E]

        def old(n):
            at3[0] += n
            return v_all[:, at3[0] - n:at3[0]]

        row_in = [old(ROW) for _ in range(4)]
        xt = pair_of(lambda s: old(D))
        gated = pair_of(lambda s: old(H))
        hidden = pair_of(lambda s: old(HP))
        hidden_t = pair_of(lambda s: old(HP))
        y_out = [old(D) for _ in range(4)]
        y_index = [sb(f"y_index{s}", [P, 1], U32) for s in range(4)]
        y_in = [arena[:, 1024 * s:1024 * s + PG * TOPK * D] for s in range(4)]

        sorted_rows = nc.dram_tensor("sorted_rows", (NULL_ROW + E * P, ROW), FP32, kind="Internal").ap()
        expert_out = nc.dram_tensor("expert_out", (TRASH + 2 * E * P, D), FP32, kind="Internal").ap()

        bank = [es.enter_context(nc.psum_tensor(f"bank{i}", [P, 512], FP32)) for i in range(8)]
        scores = [bank[0:2], bank[2:4]]
        aux = bank[7]
        AUX_O, AUX_X, AUX_L, AUX_R, AUX_T = 0, 128, 256, 320, 320 + PG * E

        const_loaded, consts_ready, tanh_ready, bo_done = sem("const_loaded"), sem("consts_ready"), sem("tanh_ready"), sem("bo_done")
        w2_loaded, w13_loaded = sem("w2_loaded"), sem("w13_loaded")
        x_loaded, c_loaded = [sem(f"x_loaded{s}") for s in range(4)], [sem(f"c_loaded{s}") for s in range(4)]
        var_ready, std_ready, xn_ready = sem("var_ready"), sem("std_ready"), sem("xn_ready")
        xt_done, xt_copied = sem("xt_done"), sem("xt_copied")
        k_done, q_done, v_done = sem("k_done"), sem("q_done"), sem("v_done")
        k_copied, q_copied, v_copied = sem("k_copied"), sem("q_copied"), sem("v_copied")
        operands_ready, values_ready = sem("operands_ready"), sem("values_ready")
        scores_done, max_ready, shifted, probs_ready = sem("scores_done"), sem("max_ready"), sem("shifted"), sem("probs_ready")
        t_done, t_copied = pair_of(lambda h: sem(f"t_done{h}")), pair_of(lambda h: sem(f"t_copied{h}"))
        av_done, o_ready = sem("av_done"), sem("o_ready")
        res_loaded = pair_of(lambda s: sem(f"res_loaded{s}"))
        x2_ready, x2_copied = sem("x2_ready"), sem("x2_copied")
        mid_done, mid_read, end_done, end_read = sem("mid_done"), sem("mid_read"), sem("end_done"), sem("end_read")
        xn2_ready, gap_ready, ratio_ready, rows_copied, rows_ready = (
            sem("xn2_ready"), sem("gap_ready"), sem("ratio_ready"), sem("rows_copied"), sem("rows_ready"))
        scattered = pair_of(lambda s: sem(f"scattered{s}"))
        pads_ready, padded, table_ready = sem("pads_ready"), sem("padded"), sem("table_ready")
        row_loaded = [sem(f"row_loaded{s}") for s in range(4)]
        row_turned, row_copied, up_done, gated_ready, hidden_ready = (
            sem("row_turned"), sem("row_copied"), sem("up_done"), sem("gated_ready"), sem("hidden_ready"))
        hidden_turned, hidden_copied, down_done, y_ready = sem("hidden_turned"), sem("hidden_copied"), sem("down_done"), sem("y_ready")
        y_sent = [sem(f"y_sent{s}") for s in range(4)]
        y_loaded, sum_ready = [sem(f"y_loaded{s}") for s in range(4)], sem("sum_ready")
        stored, wait_carried = sem("stored"), sem("wait_carried")

        x_v = x.rearrange("(n c) s d -> (c s) n d", c=2)
        out_v = out.rearrange("(n c) s d -> (c s) n d", c=2)
        y_v = expert_out[0:TRASH, :].rearrange("(n p k) d -> p n k d", p=P, k=TOPK)

        class Sweep:

            def __init__(self, units, unroll, peeled):
                self.units, self.unroll, self.peeled = units, unroll, peeled

            def __call__(self, eng, lag, step):
                assert lag <= self.peeled * self.unroll
                for m in range(self.peeled * self.unroll):
                    step(m // self.unroll, m % self.unroll)
                with eng.Fori(self.peeled, self.units // self.unroll) as i:
                    for j in range(self.unroll):
                        step(i, j)
                for m in range(self.units, self.units + lag):
                    step(m // self.unroll, m % self.unroll)

            def live(self, i, j, lag=0):
                return not isinstance(i, int) or 0 <= i * self.unroll + j - lag < self.units

            def reached(self, i, j, unit):
                assert isinstance(i, int) or self.peeled * self.unroll + j >= unit
                return not isinstance(i, int) or i * self.unroll + j >= unit

        project, attend = Sweep(GROUPS, UNROLL1, 1), Sweep(PAIRS, UNROLL2, 3)
        experts, combine = Sweep(TILES, UNROLL3, 1), Sweep(GROUPS, UNROLL4, 1)

        def blocks(v):
            return v[:, :].rearrange("p (m h e) -> p m h e", h=2, e=HD + 1)

        def group_of(i, j, lag):
            return i * (UNROLL2 // PG) + (j - lag) // PG

        N_CONST = 9 * 16
        ATTN_LAST = PAIRS + AT_TURN

        def m_or_last(m):
            return m if not isinstance(m, int) or m < ATTN_LAST else ATTN_LAST

        block = es.enter_context(nc.Block())

        @block.sync
        def _(sp):
            for dst, src in ((const_sb[:, :], consts), (bias_sb[:, :], qk_bias), (gate_sb[:, :], gates), (bv_sb[:, :], bv),
                             (bo_sb[:, :], bo), (wqkv_sb[:, :], w_qkv), (wo_sb[:, :], w_o), (wgate_sb[:, :], w_gate)):
                sp.dma_start(dst, src).then_inc(const_loaded, 16)
            sp.dma_start(w2_sb[:, :], w2).then_inc(const_loaded, 16)

            def load_step(i, j):
                s, n = j % 4, i * UNROLL1 + j
                if project.reached(i, j, 4):
                    sp.wait_ge(xt_done, n - 3)
                sp.dma_start(x_in[s].rearrange("p (q d) -> p q d", q=PG), x_v[:, bass.ds(n * PG, PG), :]).then_inc(x_loaded[s], 16)
                if project.reached(i, j, 4):
                    sp.wait_ge(v_done, n - 3)
                sp.dma_start(c_t[s], ctx[:, bass.ds(n * PG * P, PG * P)]).then_inc(c_loaded[s], 16)

            project(sp, 0, load_step)

            def residual_step(i, j):
                s, n = j % 2, i * UNROLL2 + j
                if attend.reached(i, j, 2):
                    sp.wait_ge(x2_ready, n - 1)
                sp.dma_start(x_res[s][:, :], x_v[:, bass.ds(n, 1), :].rearrange("p n d -> p (n d)")).then_inc(res_loaded[s], 16)

            sp.wait_ge(pads_ready, 4)
            sp.dma_start(sorted_rows[NULL_ROW:NULL_ROW + E * P, :].rearrange("(e p) c -> p e c", p=P), pad_rows[:, E:2 * E, :]).then_inc(padded, 16)
            attend(sp, 0, residual_step)
            sp.wait_ge(operands_ready, 2 * PAIRS)
            sp.dma_start(w13_sb, w13).then_inc(w13_loaded, 16)
            sp.wait_ge(pads_ready, 5)
            for e in range(E):
                row = sp.value_load(first_pad[0:1, e:e + 1], min_val=e * REGION, max_val=e * REGION + TOKENS)
                sp.dma_start(sorted_rows[bass.ds(row, P), :], pad_rows[:, e, :]).then_inc(padded, 16)
            sp.wait_ge(table_ready, 1)
            for s in range(2):
                sp.wait_ge(scattered[s], GROUPS // 2 * PG * TOPK * 16)
            sp.wait_ge(padded, (E + 1) * 16)

            def row_step(i, j):
                t, s = i * UNROLL3 + j, j % 4
                if experts.reached(i, j, 4):
                    sp.wait_ge(hidden_ready, t - 3)
                row = sp.value_load(tile_row[0:1, bass.ds(t, 1)], min_val=0, max_val=NULL_ROW + (E - 1) * P)
                sp.dma_start(row_in[s], sorted_rows[bass.ds(row, P), :]).then_inc(row_loaded[s], 16)

            experts(sp, 0, row_step)
            for s in range(4):
                sp.wait_ge(y_sent[s], TILES // 4 * 16)

            def y_step(i, j):
                s, n = j % 4, i * UNROLL4 + j
                if combine.reached(i, j, 4):
                    sp.wait_ge(sum_ready, n - 3)
                sp.dma_start(y_in[s].rearrange("p (n k d) -> p n k d", n=PG, k=TOPK),
                             y_v[:, bass.ds(n * PG, PG), :, :]).then_inc(y_loaded[s], 16)

            combine(sp, 0, y_step)
            sp.wait_ge(stored, GROUPS * 16)

        @block.gpsimd
        def _(pool):
            def carry_wait():
                pool.sem_inc(wait_carried, 1)

            for s in range(2):
                pool.memset(rows[s][:, :, :, :], 0.0).then_inc(pads_ready, 1)
            pool.memset(pad_rows[:, :, :], 0.0).then_inc(pads_ready, 1)
            pool.wait_ge(const_loaded, N_CONST)
            pool.wait_ge(pads_ready, 3)
            pool.tensor_copy(pad_rows[:, :, D], const(C_TRASH, 2 * E)).then_inc(pads_ready, 1)
            for s in range(2):
                pool.tensor_copy(blocks(v_blk[s])[:, :, :, HD], parity_mask.unsqueeze(1).to_broadcast([P, HEADS, 2]))
            pool.wait_ge(k_copied, GROUPS)
            pool.wait_ge(q_copied, GROUPS)
            pool.wait_ge(v_copied, GROUPS)

            def expand_step(i, j):
                s = j % 2
                if attend.live(i, j):
                    n = i * UNROLL2 + j
                    if attend.reached(i, j, 2):
                        pool.wait_ge(scores_done, n - 1)
                    k = k_all[:, bass.ds(n * 2 * S, 2 * S)].rearrange("p (t k) -> p t k", t=2)
                    q = qx_all[:, bass.ds(n * 2 * S, 2 * S)].rearrange("p (t k) -> p t k", t=2)
                    pool.tensor_tensor(k_mask[s][:, :, :, :], k.unsqueeze(2).to_broadcast([P, 2, QUAD, S]),
                                       head_mask.unsqueeze(1).unsqueeze(3).to_broadcast([P, 2, QUAD, S]), ALU.mult).then_inc(operands_ready, 1)
                    pool.tensor_tensor(q_blk[s][:, :, :, :], q.unsqueeze(2).to_broadcast([P, 2, 2, S]),
                                       batch_mask.unsqueeze(1).unsqueeze(3).to_broadcast([P, 2, 2, S]), ALU.mult).then_inc(operands_ready, 1)
                if attend.live(i, j, 2):
                    n = i * UNROLL2 + j - 2
                    if attend.reached(i, j, 4):
                        pool.wait_ge(av_done, n - 1)
                    v = v_all[:, bass.ds(n * 2 * D, 2 * D)].rearrange("p (m h d) -> p m h d", h=2, d=HD)
                    pool.tensor_tensor(blocks(v_blk[s])[:, :, :, 0:HD], v,
                                       parity_mask.unsqueeze(1).unsqueeze(3).to_broadcast([P, HEADS, 2, HD]), ALU.mult).then_inc(values_ready, 1)
                if attend.live(i, j, AT_SEND):
                    n, g, q = i * UNROLL2 + j - AT_SEND, (j - AT_SEND) // PG % 2, (j - AT_SEND) % PG
                    if q == 0:
                        pool.wait_ge(rows_ready, n + PG)
                        carry_wait()
                    for k in range(TOPK):
                        pool.indirect_dma_start(sorted_rows, bass.IndirectOffsetOnAxis(ap=index[g][:, k, q:q + 1], axis=0),
                                                rows[g][:, q, k, :], None).then_inc(scattered[g], 16)

            attend(pool, AT_SEND, expand_step)
            def send_step(i, j):
                if not experts.live(i, j, 4):
                    return
                t, s = i * UNROLL3 + j - 4, (j - 4) % 4
                pool.wait_ge(y_ready, t + 1)
                carry_wait()
                pool.indirect_dma_start(expert_out, bass.IndirectOffsetOnAxis(ap=y_index[s][:, :], axis=0),
                                        y_out[s], None).then_inc(y_sent[s], 16)

            experts(pool, 4, send_step)

        @block.vector
        def _(dve):
            dve.wait_ge(const_loaded, N_CONST)
            dve.tensor_copy(ident_r[:, :], ident)
            dve.tensor_copy(tri_r[:, :], tri)
            dve.tensor_copy(ones_r[:, :], ones)
            dve.tensor_scalar(either[:, PG, :], const(C_RANK, E), 0.0, None, ALU.mult)
            dve.tensor_copy(base[:, :], const(C_REGION, E))
            dve.tensor_copy(dest[:, :, :], const(C_DEST, PG * TOPK).rearrange("p (q k) -> p q k", q=PG))
            dve.wait_ge(bo_done, 1)
            dve.tensor_tensor(bo_sb[:, :], bank[0][0:1, 0:D], bo_sb[:, :], ALU.add)
            dve.wait_ge(tanh_ready, 1)
            dve.tensor_scalar(wo_sb[:, :], wo_sb[:, :], tanh_gate[:, 0:1], None, ALU.mult)
            dve.drain()
            dve.tensor_scalar(bo_sb[:, :], bo_sb[:, :], tanh_gate[0:1, 0:1], None, ALU.mult).then_inc(consts_ready, 1)

            def project_step(i, j):
                n = i * UNROLL1 + j
                if project.live(i, j):
                    s = j % 4
                    dve.wait_ge(x_loaded[s], (i * (UNROLL1 // 4) + j // 4 + 1) * 16)
                    for q in range(PG):
                        dve.bn_stats(stats[:, q, :], x_in[s][:, q * D:q * D + D])
                    dve.drain()
                    for q in range(PG):
                        last = dve.bn_aggr(mv[:, q, :], stats[:, q, :])
                    last.then_inc(var_ready, 1)
                if project.live(i, j):
                    s = j % 4
                    dve.wait_ge(std_ready, n + 1)
                    dve.reciprocal(rstd[:, :], std[:, :])
                    dve.drain()
                    for q in range(PG):
                        last = dve.tensor_scalar(x_in[s][:, q * D:q * D + D], x_in[s][:, q * D:q * D + D],
                                                 mv[:, q, 0:1], rstd[:, q:q + 1], ALU.subtract, ALU.mult)
                    last.then_inc(xn_ready, 1)
                if project.live(i, j, 2):
                    dve.wait_ge(v_done, n - 1)
                    for h in range(2):
                        last = dve.tensor_copy(v_all[:, bass.ds((n - 2) * 2 * D * PG + h * 512, 512)], bank[6 + h][:, :])
                    last.then_inc(v_copied, 1)

            project(dve, 2, project_step)

            def norm_guess(stage, g):
                if stage == 0:
                    for q in range(PG):
                        dve.bn_aggr(mv[:, q, :], stats[:, q, :])
                elif stage == 1:
                    dve.tensor_scalar(var[:, :], mv[:, :, 1], EPS, None, ALU.add)
                elif stage == 2:
                    dve.tensor_scalar(newton[:, :].bitcast(U32), var[:, :].bitcast(U32), 1, None, ALU.logical_shift_right)
                elif stage == 3:
                    dve.tensor_scalar(rstd[:, :].bitcast(I32), newton[:, :].bitcast(I32), -1.0, float(MAGIC), ALU.mult, ALU.add)

            def norm_refine(stage):
                if stage % 3 == 0:
                    dve.tensor_tensor(newton[:, :], rstd[:, :], rstd[:, :], ALU.mult)
                elif stage % 3 == 1:
                    dve.scalar_tensor_tensor(newton[:, :], newton[:, :], -0.5, var[:, :], ALU.mult, ALU.mult)
                else:
                    dve.scalar_tensor_tensor(rstd[:, :], newton[:, :], 1.5, rstd[:, :], ALU.add, ALU.mult)

            def norm_apply(i, j, g):
                if attend.reached(i, j, AT_NORM + 2 + 2 * PG):
                    dve.wait_ge(rows_copied, group_of(i, j, AT_NORM + 2) - 1)
                for q in range(PG):
                    last = dve.tensor_scalar(xn2g[g][:, q, :], x2g[g][:, q, :], mv[:, q, 0:1], rstd[:, q:q + 1], ALU.subtract, ALU.mult)
                last.then_inc(xn2_ready, 1)

            rank = const(C_RANK, E).unsqueeze(1).to_broadcast([P, PG, E])
            spread = lambda v: v[:, :].unsqueeze(2).to_broadcast([P, PG, E])

            def choose(stage, g):
                k = stage // 6
                left, top = (logits[g][:, :, :], best) if k == 0 else (rest[:, :, :], second)
                if stage % 6 == 0:
                    dve.tensor_reduce(top[:, :], left, AX.X, ALU.max)
                elif stage % 6 == 1:
                    dve.tensor_tensor(work[:, 0], left, spread(top), ALU.is_equal)
                elif stage % 6 == 2:
                    dve.tensor_tensor(work[:, 0], work[:, 0], rank, ALU.mult)
                elif stage % 6 == 3:
                    dve.tensor_reduce(picked[:, :], work[:, 0], AX.X, ALU.max)
                elif stage % 6 == 4:
                    dve.tensor_tensor(chosen[:, k], rank, spread(picked), ALU.is_equal)
                elif k == 0:
                    dve.scalar_tensor_tensor(rest[:, :, :], chosen[:, 0], BELOW_ALL, left, ALU.mult, ALU.add)
                else:
                    dve.tensor_tensor(either[:, 0:PG, :], chosen[:, 0], chosen[:, 1], ALU.add)
                    dve.tensor_tensor(gap[:, :], second[:, :], best[:, :], ALU.subtract).then_inc(gap_ready, 1)

            def place_rows(stage, i, j):
                if stage == 0:
                    dve.tensor_tensor(place[:, :, :], aux[:, AUX_R:AUX_R + PG * E].rearrange("p (q e) -> p q e", e=E),
                                      base[:, :].unsqueeze(1).to_broadcast([P, PG, E]), ALU.add)
                    dve.wait_ge(ratio_ready, group_of(i, j, AT_PLACE) + 1)
                    dve.tensor_scalar(share[:, :], ratio[:, :], 1.0, None, ALU.add)
                elif stage == 1:
                    dve.tensor_tensor(base[:, :], aux[:, AUX_T:AUX_T + E], base[:, :], ALU.add).then_inc(mid_read, 1)
                    for k in range(TOPK):
                        dve.tensor_tensor(work[:, k], chosen[:, k], place[:, :, :], ALU.mult)
                    dve.reciprocal(share[:, :], share[:, :])
                elif stage == 2:
                    dve.tensor_reduce(place_of[:, :, :], work[:, :, :, :], AX.X, ALU.add)
                    dve.tensor_scalar(share[:, :], share[:, :], tanh_gate[:, 1:2], None, ALU.mult)

            def fill_rows(stage, i, j):
                g = (j - AT_PLACE - 1) // PG % 2
                if stage == 0:
                    if attend.reached(i, j, AT_PLACE + 1 + 2 * PG):
                        dve.wait_ge(scattered[g], (i * (UNROLL2 // (2 * PG)) + (j - AT_PLACE - 1) // (2 * PG)) * PG * TOPK * 16)
                    dve.wait_ge(rows_copied, group_of(i, j, AT_PLACE + 1) + 1)
                    dve.tensor_copy(index[g][:, :, :], place_of[:, :, :])
                    dve.tensor_copy(rows[g][:, :, :, D], dest[:, :, :])
                    dve.tensor_copy(rows[g][:, :, 0, D + 1], share[:, :])
                    dve.tensor_tensor(rows[g][:, :, 1, D + 1], share[:, :], ratio[:, :], ALU.mult).then_inc(rows_ready, PG)
                elif stage == 1:
                    dve.tensor_scalar(dest[:, :, :], dest[:, :, :], float(PG * P * TOPK), None, ALU.add)

            def group_work(i, j):
                at = lambda lag: (j - lag) % PG == 0 and attend.live(i, j, lag)
                slot = lambda lag: (j - lag) // PG % 2
                if at(AT_CHOOSE):
                    dve.wait_ge(end_read, m_or_last(i * UNROLL2 + j) - 4)
                for stage in range(6 if at(AT_NORM + 1) else 4):
                    if at(AT_NORM):
                        norm_guess(stage, slot(AT_NORM))
                    if at(AT_NORM + 1):
                        norm_refine(stage)
                    if at(AT_NORM + 2):
                        if stage < 3:
                            norm_refine(stage)
                        else:
                            norm_apply(i, j, slot(AT_NORM + 2))
                    for quarter in range(3):
                        if at(AT_CHOOSE + quarter) and stage < 4:
                            choose(4 * quarter + stage, slot(AT_CHOOSE + quarter))
                    if at(AT_PLACE):
                        place_rows(stage, i, j)
                    if at(AT_PLACE + 1):
                        fill_rows(stage, i, j)
                    dve.drain()

            def attend_step(i, j):
                m = i * UNROLL2 + j
                if attend.live(i, j):
                    s = j % 2
                    dve.wait_ge(scores_done, m + 1)
                    if attend.reached(i, j, 2):
                        dve.wait_ge(shifted, m - 1)
                    for half in range(2):
                        last = dve.tensor_reduce(neg_max[s][:, half * 8:half * 8 + 8],
                                                 scores[s][half][:, :].rearrange("p (h k) -> p h k", k=S), AX.X, ALU.max, negate=True)
                    last.then_inc(max_ready, 1)
                x2_live, turn_live = attend.live(i, j, AT_X2), attend.live(i, j, AT_TURN)
                place_live = (j - AT_PLACE) % PG == 0 and attend.live(i, j, AT_PLACE)
                if x2_live or turn_live or place_live:
                    dve.wait_ge(mid_done, m_or_last(m) - 4)
                if turn_live:
                    last = dve.tensor_copy(xn2_t[(j - AT_TURN) % 2][:, :], aux[:, AUX_X:AUX_X + D])
                    if not x2_live and not place_live:
                        last.then_inc(mid_read, 1)
                if x2_live:
                    n, s, g, q = m - AT_X2, (j - AT_X2) % 2, (j - AT_X2) // PG % 2, (j - AT_X2) % PG
                    dve.wait_ge(res_loaded[s], (i * (UNROLL2 // 2) + (j - AT_X2) // 2 + 1) * 16)
                    if q == 0 and attend.reached(i, j, AT_X2 + 2 * PG):
                        dve.wait_ge(x2_copied, n - PG)
                    last = dve.tensor_tensor(x2g[g][:, q, :], aux[:, AUX_O:AUX_O + D], x_res[s][:, :], ALU.add)
                    last.then_inc(x2_ready, 1)
                    dve.drain()
                    last = dve.bn_stats(stats[:, q, :], x2g[g][:, q, :])
                    if not place_live:
                        last.then_inc(mid_read, 1)
                    dve.drain()
                group_work(i, j)
                if attend.live(i, j, 3):
                    n, s = m - 3, (j - 3) % 2
                    dve.wait_ge(av_done, n + 1)
                    if attend.reached(i, j, 5):
                        dve.wait_ge(end_done, n - 1)
                    halves = [(slice(64 * b, 64 * b + 64), bank[6][64 * b:64 * b + 64, 0:HEADS // 2 * VB].rearrange(
                        "p (j b h e) -> p j b h e", b=2, h=2, e=HD + 1)[:, :, b]) for b in range(2)]
                    for rows_, o in halves:
                        dve.reciprocal(rsum[rows_, :].rearrange("p (j h) -> p j h", h=2), o[:, :, :, HD])
                    dve.drain()
                    for rows_, o in halves:
                        r = rsum[rows_, :].rearrange("p (j h) -> p j h", h=2).unsqueeze(3).to_broadcast([64, HEADS // 2, 2, HD])
                        last = dve.tensor_tensor(o_buf[s][rows_, :].rearrange("p (j h d) -> p j h d", h=2, d=HD),
                                                 o[:, :, :, 0:HD], r, ALU.mult)
                    last.then_inc(o_ready, 1)

            attend(dve, AT_SEND, attend_step)

            dve.tensor_copy(first_pad[:, :], base[:, :]).then_inc(pads_ready, 1)
            dve.tensor_tensor(count[:, :], base[:, :], const(C_REGION, E), ALU.subtract)
            dve.drain()
            dve.tensor_scalar(count[:, :], count[:, :], float(P - 1), None, ALU.add)
            dve.drain()
            dve.tensor_copy(count_i[:, :], count[:, :])
            dve.drain()
            dve.tensor_scalar(count_i[:, :], count_i[:, :], 7, None, ALU.logical_shift_right)
            dve.drain()
            dve.tensor_copy(tiles_of[:, :], count_i[:, :])
            dve.drain()
            dve.tensor_scalar(skip[:, :], tiles_of[:, :], -float(P), float(REGION), ALU.mult, ALU.add)
            src = tiles_of
            for n, step in enumerate((1, 2, 4)):
                dst = upto[n % 2]
                dve.tensor_copy(dst[:, 0:step], src[:, 0:step])
                dve.tensor_tensor(dst[:, step:E], src[:, step:E], src[:, 0:E - step], ALU.add)
                dve.drain()
                src = dst
            tile = const_sb[0:1, C_TILE:C_TILE + TILES]
            dve.tensor_tensor(passed, tile.unsqueeze(2).to_broadcast([1, TILES, E]),
                              src[0:1, :].unsqueeze(1).to_broadcast([1, TILES, E]), ALU.is_ge)
            dve.drain()
            dve.tensor_tensor(skipped, passed, skip[0:1, :].unsqueeze(1).to_broadcast([1, TILES, E]), ALU.mult)
            dve.tensor_reduce(tile_f[:, 0, :], passed, AX.X, ALU.add)
            dve.drain()
            dve.tensor_reduce(tile_f[:, 1, :], skipped, AX.X, ALU.add)
            dve.tensor_scalar(tile_up[:, :], tile_f[:, 0, :], float(E - 1), float(2 * H), ALU.min, ALU.mult)
            dve.tensor_scalar(tile_down[:, :], tile_f[:, 0, :], float(E - 1), float(D), ALU.min, ALU.mult)
            dve.drain()
            dve.scalar_tensor_tensor(tile_f[:, 1, :], tile, float(P), tile_f[:, 1, :], ALU.mult, ALU.add)
            dve.drain()
            dve.tensor_copy(tile_row[:, :], tile_f[:, 1, :]).then_inc(table_ready, 1)
            for s in range(2):
                dve.memset(hidden[s][:, H:HP], 0.0)

            def expert_step(i, j):
                t = i * UNROLL3 + j
                if experts.live(i, j, 1):
                    s, s4 = (j - 1) % 2, (j - 1) % 4
                    dve.wait_ge(gated_ready, t)
                    if experts.reached(i, j, 3):
                        dve.wait_ge(hidden_turned, t - 2)
                    dve.scalar_tensor_tensor(hidden[s][:, 0:H], gated[s], row_in[s4][:, D + 1:D + 2], bank[3 + s][:, 0:H],
                                             ALU.mult, ALU.mult)
                    if experts.reached(i, j, 5):
                        use = i * (UNROLL3 // 4) + (j - 1) // 4
                        dve.wait_ge(y_sent[s4], use * 16)
                    dve.tensor_copy(y_index[s4][:, :], row_in[s4][:, D:D + 1]).then_inc(hidden_ready, 1)
                if experts.live(i, j, 3):
                    s, s4 = (j - 3) % 2, (j - 3) % 4
                    dve.wait_ge(down_done, t - 2)
                    dve.tensor_copy(y_out[s4], bank[6 + s][:, 0:D]).then_inc(y_ready, 1)

            experts(dve, 3, expert_step)

            def sum_step(i, j):
                s, n, u = j % 4, i * UNROLL4 + j, i * (UNROLL4 // 4) + j // 4
                dve.wait_ge(y_loaded[s], (u + 1) * 16)
                y = y_in[s].rearrange("p (n k d) -> p n k d", n=PG, k=TOPK)
                x2 = qx_all[:, bass.ds(n * PG * D, PG * D)].rearrange("p (n d) -> p n d", d=D)
                dve.tensor_tensor(y[:, :, 0, :], y[:, :, 0, :], y[:, :, 1, :], ALU.add)
                dve.drain()
                dve.tensor_tensor(x2, x2, y[:, :, 0, :], ALU.add).then_inc(sum_ready, 1)

            combine(dve, 0, sum_step)

        @block.scalar
        def _(act):
            act.wait_ge(const_loaded, N_CONST)
            act.activation(tanh_gate[:, :], gate_sb[:, :], ACT.Tanh).then_inc(tanh_ready, 1)

            def project_step(i, j):
                n = i * UNROLL1 + j
                if project.live(i, j):
                    act.wait_ge(var_ready, n + 1)
                    act.activation(std[:, :], mv[:, :, 1], ACT.Sqrt, bias=const(C_EPS)).then_inc(std_ready, 1)
                if project.live(i, j, 1):
                    s = (j - 1) % 2
                    act.wait_ge(xt_done, n)
                    if project.reached(i, j, 3):
                        act.wait_ge(q_done, n - 2)
                    act.copy(xn_t[s], bank[s][:, :]).then_inc(xt_copied, 1)
                if project.live(i, j, 2):
                    s = j % 2
                    for store, out_bank, bias, done, copied in ((k_all, bank[2 + s], 2, k_done, k_copied), (qx_all, bank[4 + s], 0, q_done, q_copied)):
                        act.wait_ge(done, n - 1)
                        for t in range(2):
                            dst = store[:, bass.ds((n - 2) * 2 * S * PG, 2 * S * PG)].rearrange("p (q t k) -> p q t k", q=PG, t=2)
                            last = act.activation(dst[:, :, t, :], out_bank[:, 256 * t:256 * t + 256].rearrange("p (q k) -> p q k", q=PG),
                                                  ACT.Identity, bias=bias_sb[:, bias + t:bias + t + 1])
                        last.then_inc(copied, 1)

            project(act, 2, project_step)

            def attend_step(i, j):
                m = i * UNROLL2 + j
                if (j - AT_PLACE) % PG == 0 and attend.live(i, j, AT_PLACE):
                    act.wait_ge(gap_ready, group_of(i, j, AT_PLACE) + 1)
                    act.activation(ratio[:, :], gap[:, :], ACT.Exp).then_inc(ratio_ready, 1)
                if attend.live(i, j, 1):
                    n, s = m - 1, (j - 1) % 2
                    act.wait_ge(shifted, n + 1)
                    if attend.reached(i, j, 3):
                        act.wait_ge(t_done[1], n - 1)
                    for half in range(2):
                        last = act.activation(probs[s][:, half * 512:half * 512 + 512], scores[s][half][:, :], ACT.Exp, scale=HD ** -0.5)
                    last.then_inc(probs_ready, 1)
                if attend.live(i, j, 2):
                    n, s = m - 2, j % 2
                    act.wait_ge(t_done[0], n + 1)
                    if attend.reached(i, j, 4):
                        act.wait_ge(av_done, n - 1)
                    act.copy(probs_t[s][:, 0:512], bank[4][:, :]).then_inc(t_copied[0], 1)
                    act.wait_ge(t_done[1], n + 1)
                    act.copy(probs_t[s][:, 512:1024], bank[5][:, :]).then_inc(t_copied[1], 1)
                if attend.live(i, j, 4) or attend.live(i, j, AT_TURN):
                    act.wait_ge(end_done, m - 3)
                    if attend.live(i, j, AT_TURN):
                        g, q = (j - AT_TURN) // PG % 2, (j - AT_TURN) % PG
                        last = act.copy(logits[g][:, q, :], aux[:, AUX_L:AUX_L + E])
                    if attend.live(i, j, 4):
                        if attend.reached(i, j, 6):
                            act.wait_ge(mid_done, m - 5)
                        last = act.copy(o_t[(j - 4) % 2][:, :], aux[:, AUX_O:AUX_O + D])
                    last.then_inc(end_read, 1)
                if attend.live(i, j, AT_X2 + 1):
                    n, g, q = m - AT_X2 - 1, (j - AT_X2 - 1) // PG % 2, (j - AT_X2 - 1) % PG
                    act.wait_ge(x2_ready, n + 1)
                    act.copy(qx_all[:, bass.ds(n * D, D)], x2g[g][:, q, :]).then_inc(x2_copied, 1)
                if (j - AT_COPY) % PG == 0 and attend.live(i, j, AT_COPY):
                    g = (j - AT_COPY) // PG % 2
                    if attend.reached(i, j, AT_COPY + 2 * PG):
                        act.wait_ge(scattered[g], (i * (UNROLL2 // (2 * PG)) + (j - AT_COPY) // (2 * PG)) * PG * TOPK * 16)
                    act.wait_ge(xn2_ready, group_of(i, j, AT_COPY) + 1)
                    act.copy(rows[g][:, :, :, 0:D], xn2g[g][:, :, :].unsqueeze(2).to_broadcast([P, PG, TOPK, D])).then_inc(rows_copied, 1)

            attend(act, AT_SEND, attend_step)

            def expert_step(i, j):
                t = i * UNROLL3 + j
                if experts.live(i, j):
                    s = j % 2
                    act.wait_ge(row_turned, t + 1)
                    if experts.reached(i, j, 2):
                        act.wait_ge(up_done, t - 1)
                    act.copy(xt[s], bank[0][:, 0:D]).then_inc(row_copied, 1)
                if experts.live(i, j, 1):
                    s = (j - 1) % 2
                    act.wait_ge(up_done, t)
                    if experts.reached(i, j, 3):
                        act.wait_ge(hidden_ready, t - 2)
                    act.activation(gated[s], bank[1 + s][:, 0:H], ACT.Silu).then_inc(gated_ready, 1)
                if experts.live(i, j, 2):
                    s = j % 2
                    act.wait_ge(hidden_turned, t - 1)
                    if experts.reached(i, j, 4):
                        act.wait_ge(down_done, t - 3)
                    act.copy(hidden_t[s], bank[5][:, 0:HP]).then_inc(hidden_copied, 1)

            experts(act, 2, expert_step)

            def store_step(i, j):
                n = i * UNROLL4 + j
                act.wait_ge(sum_ready, n + 1)
                act.dma_start(out_v[:, bass.ds(n * PG, PG), :],
                              qx_all[:, bass.ds(n * PG * D, PG * D)].rearrange("p (n d) -> p n d", d=D)).then_inc(stored, 16)

            combine(act, 0, store_step)

        @block.tensor
        def _(pe):
            pe.wait_ge(const_loaded, N_CONST)
            pe.matmul(bank[0][0:1, 0:D], bv_sb[:, :], wo_sb[:, :], start=True, stop=True).then_inc(bo_done, 1)
            pe.wait_ge(consts_ready, 1)

            def project_step(i, j):
                m = i * UNROLL1 + j
                if project.live(i, j, 1):
                    s = (j - 1) % 2
                    pe.wait_ge(xn_ready, m)
                    if project.reached(i, j, 3):
                        pe.wait_ge(xt_copied, m - 2)
                    for q in range(PG):
                        last = pe.transpose(bank[s][:, q * D:q * D + D], x_in[(j - 1) % 4][:, q * D:q * D + D], ident)
                    last.then_inc(xt_done, 1)
                if project.live(i, j, 2):
                    n, s, s4, u = m - 2, j % 2, (j - 2) % 4, i * (UNROLL1 // 4) + (j - 2) // 4
                    pe.wait_ge(c_loaded[s4], (u + 1) * 16)
                    for src, w0, out_bank, ready, free, done in ((c_t[s4], D, bank[2 + s], None, k_copied, k_done),
                                                                 (xn_t[s], 0, bank[4 + s], xt_copied, q_copied, q_done)):
                        if ready is not None:
                            pe.wait_ge(ready, n + 1)
                        if project.reached(i, j, 4):
                            pe.wait_ge(free, n - 1)
                        rhs = src.rearrange("p (q b k) -> p b q k", q=PG, b=2)
                        for t in range(2):
                            for half in range(2):
                                for b in range(2):
                                    c = 64 * half + 32 * b
                                    f = w0 + 64 * half + 32 * t
                                    last = pe.matmul(out_bank[c:c + 32, 256 * t:256 * t + 256], wqkv_sb[:, f:f + 32], rhs[:, b],
                                                     start=True, stop=True)
                        last.then_inc(done, 1)
                    if project.reached(i, j, 3):
                        pe.wait_ge(v_copied, n)
                    for q in range(PG):
                        for b in range(2):
                            for h in range(2):
                                last = pe.matmul(bank[6 + q // 2][64 * h:64 * h + 64, (q % 2 * 2 + b) * D:(q % 2 * 2 + b + 1) * D],
                                                 c_t[s4][:, (2 * q + b) * S:(2 * q + b + 1) * S], wqkv_sb[:, 2 * D:3 * D],
                                                 start=True, stop=True)
                    last.then_inc(v_done, 1)

            project(pe, 2, project_step)
            pe.wait_ge(k_copied, GROUPS)
            pe.wait_ge(q_copied, GROUPS)
            pe.wait_ge(v_copied, GROUPS)

            def attend_step(i, j):
                m = i * UNROLL2 + j
                if attend.live(i, j):
                    s = j % 2
                    pe.wait_ge(operands_ready, 2 * m + 2)
                    if attend.reached(i, j, 2):
                        pe.wait_ge(probs_ready, m - 1)
                    for t in range(2):
                        for half in range(2):
                            last = pe.matmul(scores[s][half][:, 256 * t:256 * t + 256],
                                             q_blk[s][64 * half:64 * half + 64, t, :, :],
                                             k_mask[s][64 * half:64 * half + 64, t, :, :],
                                             start=t == 0, stop=t == 1, skip_group_check=True)
                    last.then_inc(scores_done, 1)
                x2_live, turn_live = attend.live(i, j, AT_X2), attend.live(i, j, AT_TURN)
                place_live = (j - AT_PLACE) % PG == 0 and attend.live(i, j, AT_PLACE)
                if x2_live or turn_live or place_live:
                    pe.wait_ge(end_read, m_or_last(m) - 4)
                    if turn_live:
                        g, q = (j - AT_TURN) // PG % 2, (j - AT_TURN) % PG
                        if q == 0:
                            pe.wait_ge(xn2_ready, group_of(i, j, AT_TURN) + 1)
                        last = pe.transpose(aux[:, AUX_X:AUX_X + D], xn2g[g][:, q, :], ident)
                    if x2_live:
                        s = (j - AT_X2) % 2
                        pe.matmul(aux[:, AUX_O:AUX_O + D], o_t[s][:, :], wo_sb[:, :], start=True, stop=False)
                        last = pe.matmul(aux[:, AUX_O:AUX_O + D], ones[0:1, :], bo_sb[0:1, :], start=False, stop=True)
                    if place_live:
                        pe.wait_ge(gap_ready, group_of(i, j, AT_PLACE) + 1)
                        pe.matmul(aux[:, AUX_R:AUX_T + E], tri_r[:, :], either[:, :, :], start=True, stop=False, skip_group_check=True)
                        for q in range(PG):
                            last = pe.matmul(aux[:, AUX_R + (q + 1) * E:AUX_T + E], ones_r[:, :],
                                             either[:, q:q + 1, :].to_broadcast([P, PG - q, E]), start=False, stop=q == PG - 1,
                                             skip_group_check=True)
                    last.then_inc(mid_done, 1)
                if attend.live(i, j, 1):
                    n, s = m - 1, (j - 1) % 2
                    pe.wait_ge(max_ready, n + 1)
                    for half in range(2):
                        last = pe.matmul(scores[s][half][:, :], ident_r[:, :],
                                         neg_max[s][:, half * 8:half * 8 + 8].unsqueeze(2).to_broadcast([P, 8, S]),
                                         start=False, stop=True, skip_group_check=True)
                    last.then_inc(shifted, 1)
                if attend.live(i, j, 2):
                    n, s = m - 2, (j - 2) % 2
                    pe.wait_ge(probs_ready, n + 1)
                    for half in range(2):
                        if attend.reached(i, j, 3):
                            pe.wait_ge(t_copied[half], n)
                        for c in range(4):
                            last = pe.transpose(bank[4 + half][:, c * P:c * P + P], probs[s][:, half * 512 + c * P:half * 512 + c * P + P], ident)
                        last.then_inc(t_done[half], 1)
                if attend.live(i, j, 3):
                    n, s = m - 3, (j - 3) % 2
                    pe.wait_ge(values_ready, n + 1)
                    if attend.reached(i, j, 4):
                        pe.wait_ge(o_ready, n)
                    v_pair = v_blk[s][:, :].rearrange("p (b j c) -> p b j c", b=2, j=HEADS // 2)
                    for half in range(2):
                        pe.wait_ge(t_copied[half], n + 1)
                        for c in range(4):
                            p = half * 4 + c
                            last = pe.matmul(bank[6][:, p * VB:p * VB + VB], probs_t[s][:, p * P:p * P + P],
                                             v_pair[:, :, p], start=True, stop=True)
                    last.then_inc(av_done, 1)
                if attend.live(i, j, 4) or attend.live(i, j, AT_TURN):
                    if attend.reached(i, j, 5):
                        pe.wait_ge(mid_read, m - 4)
                    if attend.live(i, j, AT_TURN):
                        last = pe.matmul(aux[:, AUX_L:AUX_L + E], xn2_t[(j - AT_TURN) % 2][:, :], wgate_sb[:, :], start=True, stop=True)
                    if attend.live(i, j, 4):
                        pe.wait_ge(o_ready, m - 3)
                        last = pe.transpose(aux[:, AUX_O:AUX_O + D], o_buf[j % 2][:, :], ident)
                    last.then_inc(end_done, 1)

            attend(pe, AT_SEND, attend_step)
            pe.wait_ge(table_ready, 1)
            pe.wait_ge(w13_loaded, 16)

            def expert_step(i, j):
                t = i * UNROLL3 + j
                if experts.live(i, j, 1):
                    up_at = pe.value_load(tile_up[0:1, bass.ds(t - 1, 1)], min_val=0, max_val=(E - 1) * 2 * H)
                if experts.live(i, j, 3):
                    down_at = pe.value_load(tile_down[0:1, bass.ds(t - 3, 1)], min_val=0, max_val=(E - 1) * D)
                if experts.live(i, j):
                    u = i * (UNROLL3 // 4) + j // 4
                    pe.wait_ge(row_loaded[j % 4], (u + 1) * 16)
                    if experts.reached(i, j, 1):
                        pe.wait_ge(row_copied, t)
                    pe.transpose(bank[0][:, 0:D], row_in[j % 4][:, 0:D], ident).then_inc(row_turned, 1)
                if experts.live(i, j, 1):
                    s = (j - 1) % 2
                    pe.wait_ge(row_copied, t)
                    if experts.reached(i, j, 3):
                        pe.wait_ge(hidden_ready, t - 2)
                    for k in range(2):
                        last = pe.matmul(bank[1 + 2 * k + s][:, 0:H], xt[s], w13_sb[:, bass.ds(up_at + k * H, H)], start=True, stop=True)
                    last.then_inc(up_done, 1)
                if experts.live(i, j, 2):
                    s = j % 2
                    pe.wait_ge(hidden_ready, t - 1)
                    if experts.reached(i, j, 3):
                        pe.wait_ge(hidden_copied, t - 2)
                    for c in range(CHUNKS):
                        last = pe.transpose(bank[5][:, c * P:c * P + P], hidden[s][:, c * P:c * P + P], ident)
                    last.then_inc(hidden_turned, 1)
                if experts.live(i, j, 3):
                    s = (j - 3) % 2
                    pe.wait_ge(hidden_copied, t - 2)
                    if experts.reached(i, j, 5):
                        pe.wait_ge(y_ready, t - 4)
                    for c in range(CHUNKS):
                        last = pe.matmul(bank[6 + s][:, 0:D], hidden_t[s][:, c * P:c * P + P],
                                         w2_sb[:, bass.ds(down_at + c * E * D, D)], start=c == 0, stop=c == CHUNKS - 1)
                    last.then_inc(down_done, 1)

            experts(pe, 3, expert_step)


def constants():
    import numpy as np
    p = np.arange(P)
    columns = [np.eye(P), np.triu(np.ones((P, P)), 1), np.ones((P, P)),
               (p // HD % QUAD)[:, None] == np.arange(QUAD)[None],
               (p // 32 % 2)[:, None] == np.arange(2)[None],
               (p // S)[:, None] == np.arange(2)[None],
               np.full((P, 1), EPS),
               np.tile(E - np.arange(E), (P, 1)),
               np.tile(REGION * np.arange(E), (P, 1)),
               TOPK * (P * (np.arange(PG * TOPK) // TOPK)[None] + p[:, None]) + (np.arange(PG * TOPK) % TOPK)[None],
               TRASH + P * np.arange(2 * E)[None] + p[:, None],
               np.tile(np.arange(TILES), (P, 1))]
    return np.concatenate([np.asarray(c, np.float32) for c in columns], axis=1)


def kernel(**inputs):
    import numpy as np
    import concourse.bacc as bacc
    from concourse import mybir
    from concourse.bass_utils import run_bass_kernel_spmd

    p = np.arange(P)
    feature = [64 * (p // 64) + 32 * t + p % 32 for t in range(2)]
    bq, bkv = inputs["L0_xattn_bq"], inputs["L0_xattn_bkv"]
    w1, w3, w2 = inputs["L0_ffn_w1"], inputs["L0_ffn_w3"], inputs["L0_ffn_w2"]
    w13 = np.concatenate([w1.transpose(2, 0, 1), w3.transpose(2, 0, 1)], axis=2).reshape(D, E * 2 * H)
    w2p = np.pad(w2.transpose(2, 0, 1), ((0, HP - H), (0, 0), (0, 0)))
    w2p = w2p.reshape(CHUNKS, P, E * D).transpose(1, 0, 2).reshape(P, CHUNKS * E * D)
    arrays = {
        "x": inputs["x"],
        "ctx": inputs["ctx_1024"].reshape(TOKENS, D).T,
        "consts": constants(),
        "qk_bias": np.stack([bq[feature[0]], bq[feature[1]], bkv[:D][feature[0]], bkv[:D][feature[1]]], axis=1),
        "gates": np.concatenate([np.broadcast_to(inputs["g_xattn"], (P, 1)), np.broadcast_to(inputs["g_ffn"], (P, 1))], axis=1),
        "bv": bkv[D:].reshape(P, 1),
        "bo": inputs["L0_xattn_bo"].reshape(1, D),
        "w_qkv": np.concatenate([inputs["L0_xattn_Wq"], inputs["L0_xattn_Wkv"]], axis=1),
        "w_o": inputs["L0_xattn_Wo"],
        "w_gate": inputs["L0_ffn_gate_w"].T,
        "w13": w13,
        "w2": w2p,
    }
    arrays = {n: np.ascontiguousarray(a) for n, a in arrays.items()}
    nc = bacc.Bacc("TRN2", target_bir_lowering=False, num_devices=1)
    args = [nc.dram_tensor("in_" + n, a.shape, mybir.dt.from_np(a.dtype), kind="ExternalInput").ap() for n, a in arrays.items()]
    out = nc.dram_tensor("out", (B, S, D), mybir.dt.from_np(np.dtype("float32")), kind="ExternalOutput").ap()
    build(nc, *args, out)
    r = run_bass_kernel_spmd(nc, [{"in_" + n: a for n, a in arrays.items()}], core_ids=[0])
    return r.results[0]["out"]
```

```python
from contextlib import ExitStack

import concourse.bass as bass
from concourse import mybir

FP32 = mybir.dt.float32
FP32R = mybir.dt.float32r
U32 = mybir.dt.uint32
I32 = mybir.dt.int32
ALU = mybir.AluOpType
ACT = mybir.ActivationFunctionType
AX = mybir.AxisListType

B, S, D = 128, 64, 128
HEADS = 16
HD = D // HEADS
P = 128
TOKENS = B * S
PAIRS = TOKENS // P
PG = 4
GROUPS = PAIRS // PG
QUAD = 4
EPS = 1e-5
UNROLL1, UNROLL2, UNROLL3, UNROLL4 = 4, 8, 8, 4
AT_X2, AT_NORM, AT_TURN, AT_CHOOSE, AT_COPY, AT_PLACE, AT_SEND = 5, 8, 11, 15, 17, 18, 20

E, H, TOPK = 8, 352, 2
CHUNKS = 3
HP = CHUNKS * P
REGION = TOKENS + P
NULL_ROW = E * REGION
ROW = D + 4
TRASH = TOPK * TOKENS
TILES = TOPK * TOKENS // P + E
BELOW_ALL = -3e38
MAGIC = 0x5F3759DF

C_IDENT, C_TRI, C_ONES = 0, P, 2 * P
C_HEAD = 3 * P
C_BATCH = C_HEAD + QUAD
C_PARITY = C_BATCH + 2
C_SUM = C_PARITY + 2
C_EPS = C_SUM + 64
C_RANK = C_EPS + 1
C_REGION = C_RANK + E
C_DEST = C_REGION + E
C_TRASH = C_DEST + PG * TOPK
C_TILE = C_TRASH + 2 * E
C_END = C_TILE + TILES


def build(nc, x, ctx, consts, qk_bias, gates, bv, bo, w_qkv, w_o, w_gate, w13, w2, out):
    es = ExitStack()
    with es:
        sb = lambda name, shape, dt=FP32: es.enter_context(nc.sbuf_tensor(name, shape, dt))
        sem = lambda name: es.enter_context(nc.semaphore(name))
        pair_of = lambda make: [make(0), make(1)]

        const_sb = sb("const_sb", [P, C_END])
        const = lambda at, n=1: const_sb[:, at:at + n]
        ident, tri, ones = const(C_IDENT, P), const(C_TRI, P), const(C_ONES, P)
        head_mask = const(C_HEAD, QUAD)
        batch_mask = const(C_BATCH, 2)
        parity_mask = const(C_PARITY, 2)
        ident_r = sb("ident_r", [P, P], FP32R)
        tri_r = sb("tri_r", [P, P], FP32R)
        ones_r = sb("ones_r", [P, P], FP32R)
        bias_sb = sb("bias_sb", [P, 4])
        gate_sb = sb("gate_sb", [P, 2])
        tanh_gate = sb("tanh_gate", [P, 2])
        bv_sb = sb("bv_sb", [P, 1])
        bo_sb = sb("bo_sb", [1, D])
        wqkv_sb = sb("wqkv_sb", [P, 3 * D])
        wo_sb = sb("wo_sb", [P, D])
        wgate_sb = sb("wgate_sb", [P, E])
        w2_sb = sb("w2_sb", [P, CHUNKS * E * D])

        qx_all = sb("qx_all", [P, PAIRS * 2 * S])
        with ExitStack() as early:
            k_all = early.enter_context(nc.sbuf_tensor("k_all", [P, PAIRS * 2 * S], FP32))
            v_all = early.enter_context(nc.sbuf_tensor("v_all", [P, PAIRS * 2 * D], FP32))
        w13_sb = sb("w13_sb", [P, E * 2 * H])
        table_room = sb("table_room", [P, PAIRS * 2 * S - E * 2 * H])
        w13_high, w13_rest = sb("w13_high", [P, E * 2 * H], FP32R), sb("w13_rest", [P, E * 2 * H], FP32R)
        xt_high = pair_of(lambda s: sb(f"xt_high{s}", [P, D], FP32R))
        xt_rest = pair_of(lambda s: sb(f"xt_rest{s}", [P, D], FP32R))
        late = sb("late", [P, PAIRS * 2 * D - 4 * E * H - 4 * D])

        arena = sb("arena", [P, 5120])
        x_in = [arena[:, 512 * s:512 * s + 512] for s in range(4)]
        c_t = [arena[:, 2048 + 512 * s:2560 + 512 * s] for s in range(4)]
        xn_t = pair_of(lambda s: arena[:, 4096 + 512 * s:4608 + 512 * s])
        probs = pair_of(lambda s: arena[:, 1024 * s:1024 * s + 1024])
        probs_t = pair_of(lambda s: arena[:, 2048 + 1024 * s:3072 + 1024 * s])
        k_mask = pair_of(lambda s: sb(f"k_mask{s}", [P, 2, QUAD, S]))
        q_blk = pair_of(lambda s: sb(f"q_blk{s}", [P, 2, 2, S]))
        v_blk = pair_of(lambda s: sb(f"v_blk{s}", [P, 2 * HEADS // 2 * 32]))
        neg_max = pair_of(lambda s: sb(f"neg_max{s}", [P, HEADS], FP32R))
        rsum = sb("rsum", [P, P])
        o_t = pair_of(lambda s: sb(f"o_t{s}", [P, D]))
        x_res = [arena[:, 4608 + D * s:4608 + D * s + D] for s in range(4)]
        bo_all = arena[:, 4480:4480 + D]
        stats = sb("stats", [P, PG, 6])
        mv = sb("mv", [P, PG, 2])
        std = sb("std", [P, PG])
        rstd = sb("rstd", [P, PG])
        var = sb("var", [P, PG])
        newton = sb("newton", [P, PG])
        x2g = pair_of(lambda s: sb(f"x2g{s}", [P, PG, D]))
        xn2g = pair_of(lambda s: sb(f"xn2g{s}", [P, PG, D]))
        xn2_t = pair_of(lambda s: sb(f"xn2_t{s}", [P, D]))
        logits = pair_of(lambda s: sb(f"logits{s}", [P, PG, E]))
        best = sb("best", [P, PG])
        second = sb("second", [P, PG])
        picked = sb("picked", [P, PG])
        rest = sb("rest", [P, PG, E])
        work = sb("work", [P, TOPK, PG, E])
        chosen = sb("chosen", [P, TOPK, PG, E])
        either = sb("either", [P, PG + 1, E], FP32R)
        gap = sb("gap", [P, PG])
        ratio = sb("ratio", [P, PG])
        share = sb("share", [P, PG])
        place = sb("place", [P, PG, E])
        place_of = sb("place_of", [P, TOPK, PG])
        index = pair_of(lambda s: sb(f"index{s}", [P, TOPK, PG], U32))
        base = sb("base", [P, E])
        dest = sb("dest", [P, PG, TOPK])
        rows = pair_of(lambda s: sb(f"rows{s}", [P, PG, TOPK, ROW]))
        pad_rows = sb("pad_rows", [P, 2 * E, ROW])
        first_pad = sb("first_pad", [P, E], I32)

        count = sb("count", [P, E])
        count_i = sb("count_i", [P, E], I32)
        tiles_of = sb("tiles_of", [P, E])
        upto = pair_of(lambda s: sb(f"upto{s}", [P, E]))
        skip = sb("skip", [P, E])
        passed = table_room[0:1, 0:TILES * E].rearrange("p (t e) -> p t e", e=E)
        skipped = table_room[0:1, TILES * E:2 * TILES * E].rearrange("p (t e) -> p t e", e=E)
        tile_f = arena[0:1, 4096:4096 + 2 * TILES].rearrange("p (k t) -> p k t", k=2)
        tile_row = sb("tile_row", [1, TILES], I32)
        tile_expert = sb("tile_expert", [1, TILES], I32)

        late_at = [0]

        def late_cols(n):
            late_at[0] += n
            return late[:, late_at[0] - n:late_at[0]]

        row_in = [late_cols(ROW) for _ in range(4)]
        gated = pair_of(lambda s: late_cols(H))
        hidden = pair_of(lambda s: late_cols(HP))
        hidden_t = pair_of(lambda s: late_cols(HP))
        y_out = [late_cols(D) for _ in range(4)]
        y_index = [sb(f"y_index{s}", [P, 1], U32) for s in range(4)]
        y_in = [arena[:, 1024 * s:1024 * s + PG * TOPK * D] for s in range(4)]

        sorted_rows = nc.dram_tensor("sorted_rows", (NULL_ROW + E * P, ROW), FP32, kind="Internal").ap()
        expert_out = nc.dram_tensor("expert_out", (TRASH + 2 * E * P, D), FP32, kind="Internal").ap()

        bank = [es.enter_context(nc.psum_tensor(f"bank{i}", [P, 512], FP32)) for i in range(8)]
        scores = [bank[0:2], bank[2:4]]
        aux = bank[7]
        AUX_O, AUX_X, AUX_L, AUX_R, AUX_T = 0, 128, 256, 320, 320 + PG * E

        const_loaded, consts_ready, tanh_ready, bo_done = sem("const_loaded"), sem("consts_ready"), sem("tanh_ready"), sem("bo_done")
        w13_loaded, rest_ready, high_ready, w2_loaded = sem("w13_loaded"), sem("rest_ready"), sem("high_ready"), sem("w2_loaded")
        x_loaded, c_loaded = [sem(f"x_loaded{s}") for s in range(4)], [sem(f"c_loaded{s}") for s in range(4)]
        var_ready, std_ready, xn_ready = sem("var_ready"), sem("std_ready"), sem("xn_ready")
        xt_done, xt_copied = sem("xt_done"), sem("xt_copied")
        k_done, q_done, v_done = sem("k_done"), sem("q_done"), sem("v_done")
        k_copied, q_copied, v_copied = sem("k_copied"), sem("q_copied"), sem("v_copied")
        operands_ready, values_ready = sem("operands_ready"), sem("values_ready")
        scores_done, max_ready, shifted, probs_ready = sem("scores_done"), sem("max_ready"), sem("shifted"), sem("probs_ready")
        t_done, t_copied = pair_of(lambda h: sem(f"t_done{h}")), pair_of(lambda h: sem(f"t_copied{h}"))
        av_done, o_ready = sem("av_done"), sem("o_ready")
        res_loaded, res_ready, bo_spread, bo_all_ready = [sem(f"res_loaded{s}") for s in range(4)], sem("res_ready"), sem("bo_spread"), sem("bo_all_ready")
        x2_ready, x2_copied = sem("x2_ready"), sem("x2_copied")
        mid_done, mid_read, end_done, end_read = sem("mid_done"), sem("mid_read"), sem("end_done"), sem("end_read")
        xn2_ready, gap_ready, ratio_ready, rows_copied, rows_ready = (
            sem("xn2_ready"), sem("gap_ready"), sem("ratio_ready"), sem("rows_copied"), sem("rows_ready"))
        scattered = pair_of(lambda s: sem(f"scattered{s}"))
        pads_ready, padded, table_ready = sem("pads_ready"), sem("padded"), sem("table_ready")
        row_loaded = [sem(f"row_loaded{s}") for s in range(4)]
        row_rest = sem("row_rest")
        row_turned, row_copied, up_done, gated_ready, hidden_ready = (
            sem("row_turned"), sem("row_copied"), sem("up_done"), sem("gated_ready"), sem("hidden_ready"))
        hidden_turned, hidden_copied, down_done, y_ready = sem("hidden_turned"), sem("hidden_copied"), sem("down_done"), sem("y_ready")
        y_sent = [sem(f"y_sent{s}") for s in range(4)]
        y_loaded, sum_ready = [sem(f"y_loaded{s}") for s in range(4)], sem("sum_ready")
        stored, wait_carried = sem("stored"), sem("wait_carried")
        blocks_cleared = sem("blocks_cleared")

        x_v = x.rearrange("(n c) s d -> (c s) n d", c=2)
        out_v = out.rearrange("(n c) s d -> (c s) n d", c=2)
        y_v = expert_out[0:TRASH, :].rearrange("(n p k) d -> p n k d", p=P, k=TOPK)

        class Sweep:

            def __init__(self, units, unroll, peeled):
                self.units, self.unroll, self.peeled = units, unroll, peeled

            def __call__(self, eng, lag, step):
                assert lag <= self.peeled * self.unroll
                for m in range(self.peeled * self.unroll):
                    step(m // self.unroll, m % self.unroll)
                with eng.Fori(self.peeled, self.units // self.unroll) as i:
                    for j in range(self.unroll):
                        step(i, j)
                for m in range(self.units, self.units + lag):
                    step(m // self.unroll, m % self.unroll)

            def live(self, i, j, lag=0):
                return not isinstance(i, int) or 0 <= i * self.unroll + j - lag < self.units

            def reached(self, i, j, unit):
                assert isinstance(i, int) or self.peeled * self.unroll + j >= unit
                return not isinstance(i, int) or i * self.unroll + j >= unit

        project, attend = Sweep(GROUPS, UNROLL1, 1), Sweep(PAIRS, UNROLL2, 3)
        experts, combine = Sweep(TILES, UNROLL3, 1), Sweep(GROUPS, UNROLL4, 1)

        def group_of(i, j, lag):
            return i * (UNROLL2 // PG) + (j - lag) // PG

        N_CONST = 8 * 16
        ATTN_LAST = PAIRS + AT_TURN

        def m_or_last(m):
            return m if not isinstance(m, int) or m < ATTN_LAST else ATTN_LAST

        block = es.enter_context(nc.Block())

        @block.sync
        def _(sp):
            for dst, src in ((const_sb[:, :], consts), (bias_sb[:, :], qk_bias), (gate_sb[:, :], gates), (bv_sb[:, :], bv),
                             (bo_sb[:, :], bo), (wqkv_sb[:, :], w_qkv), (wo_sb[:, :], w_o), (wgate_sb[:, :], w_gate)):
                sp.dma_start(dst, src).then_inc(const_loaded, 16)

            def load_step(i, j):
                s, n = j % 4, i * UNROLL1 + j
                if project.reached(i, j, 4):
                    sp.wait_ge(xt_done, n - 3)
                sp.dma_start(x_in[s].rearrange("p (q d) -> p q d", q=PG), x_v[:, bass.ds(n * PG, PG), :]).then_inc(x_loaded[s], 16)
                if project.reached(i, j, 4):
                    sp.wait_ge(v_done, n - 3)
                sp.dma_start(c_t[s], ctx[:, bass.ds(n * PG * P, PG * P)]).then_inc(c_loaded[s], 16)

            project(sp, 0, load_step)

            sp.dma_start(w2_sb[:, :], w2).then_inc(w2_loaded, 16)
            sp.wait_ge(q_done, GROUPS)

            def residual_step(i, j):
                s, n = j % 4, i * UNROLL2 + j
                if attend.reached(i, j, 4):
                    sp.wait_ge(x2_ready, n - 3)
                sp.dma_start(x_res[s], x_v[:, bass.ds(n, 1), :].rearrange("p n d -> p (n d)")).then_inc(res_loaded[s], 16)

            sp.wait_ge(pads_ready, 4)
            sp.dma_start(sorted_rows[NULL_ROW:NULL_ROW + E * P, :].rearrange("(e p) c -> p e c", p=P), pad_rows[:, E:2 * E, :]).then_inc(padded, 16)
            attend(sp, 0, residual_step)
            sp.wait_ge(operands_ready, 2 * PAIRS)
            sp.dma_start(w13_sb[:, :], w13).then_inc(w13_loaded, 16)
            sp.wait_ge(pads_ready, 5)
            for e in range(E):
                row = sp.value_load(first_pad[0:1, e:e + 1], min_val=e * REGION, max_val=e * REGION + TOKENS)
                sp.dma_start(sorted_rows[bass.ds(row, P), :], pad_rows[:, e, :]).then_inc(padded, 16)
            sp.wait_ge(table_ready, 1)
            for s in range(2):
                sp.wait_ge(scattered[s], GROUPS // 2 * PG * TOPK * 16)
            sp.wait_ge(padded, (E + 1) * 16)

            def row_step(i, j):
                t, s = i * UNROLL3 + j, j % 4
                if experts.reached(i, j, 4):
                    sp.wait_ge(hidden_ready, t - 3)
                row = sp.value_load(tile_row[0:1, bass.ds(t, 1)], min_val=0, max_val=NULL_ROW + (E - 1) * P)
                sp.dma_start(row_in[s], sorted_rows[bass.ds(row, P), :]).then_inc(row_loaded[s], 16)

            experts(sp, 0, row_step)
            for s in range(4):
                sp.wait_ge(y_sent[s], TILES // 4 * 16)

            def y_step(i, j):
                s, n = j % 4, i * UNROLL4 + j
                if combine.reached(i, j, 4):
                    sp.wait_ge(sum_ready, n - 3)
                sp.dma_start(y_in[s].rearrange("p (n k d) -> p n k d", n=PG, k=TOPK),
                             y_v[:, bass.ds(n * PG, PG), :, :]).then_inc(y_loaded[s], 16)

            combine(sp, 0, y_step)
            sp.wait_ge(stored, GROUPS * 16)

        @block.gpsimd
        def _(pool):
            def carry_wait():
                pool.sem_inc(wait_carried, 1)

            for s in range(2):
                pool.memset(rows[s][:, :, :, :], 0.0).then_inc(pads_ready, 1)
                pool.memset(v_blk[s][:, :], 0.0).then_inc(blocks_cleared, 1)
            pool.memset(pad_rows[:, :, :], 0.0).then_inc(pads_ready, 1)
            pool.wait_ge(const_loaded, N_CONST)
            pool.wait_ge(pads_ready, 3)
            pool.tensor_copy(pad_rows[:, :, D], const(C_TRASH, 2 * E)).then_inc(pads_ready, 1)
            pool.wait_ge(k_copied, GROUPS)
            pool.wait_ge(q_copied, GROUPS)
            pool.wait_ge(v_copied, GROUPS)
            pool.wait_ge(bo_all_ready, 1)
            pool.wait_ge(blocks_cleared, 2)

            def expand_step(i, j):
                s = j % 2
                if attend.live(i, j):
                    n = i * UNROLL2 + j
                    if attend.reached(i, j, 2):
                        pool.wait_ge(scores_done, n - 1)
                    k = k_all[:, bass.ds(n * 2 * S, 2 * S)].rearrange("p (t k) -> p t k", t=2)
                    q = qx_all[:, bass.ds(n * 2 * S, 2 * S)].rearrange("p (t k) -> p t k", t=2)
                    pool.tensor_tensor(k_mask[s][:, :, :, :], k.unsqueeze(2).to_broadcast([P, 2, QUAD, S]),
                                       head_mask.unsqueeze(1).unsqueeze(3).to_broadcast([P, 2, QUAD, S]), ALU.mult).then_inc(operands_ready, 1)
                    pool.tensor_tensor(q_blk[s][:, :, :, :], q.unsqueeze(2).to_broadcast([P, 2, 2, S]),
                                       batch_mask.unsqueeze(1).unsqueeze(3).to_broadcast([P, 2, 2, S]), ALU.mult).then_inc(operands_ready, 1)
                if attend.live(i, j, 2):
                    n = i * UNROLL2 + j - 2
                    if attend.reached(i, j, 4):
                        pool.wait_ge(av_done, n - 1)
                    v = v_all[:, bass.ds(n * 2 * D, 2 * D)].rearrange("p (m c) -> p m c", c=32)
                    for r in range(2):
                        pool.tensor_tensor(v_blk[s][:, :].rearrange("p (m c) -> p m c", c=64)[:, :, 48 * r:48 * r + 16].rearrange("p m (h d) -> p m h d", h=2),
                                           v[:, :, 16 * r:16 * r + 16].rearrange("p m (h d) -> p m h d", h=2),
                                           parity_mask.unsqueeze(1).unsqueeze(3).to_broadcast([P, 8, 2, HD]), ALU.mult).then_inc(values_ready, 1)
                if attend.live(i, j, AT_X2 - 1):
                    s = (j - AT_X2 + 1) % 4
                    pool.wait_ge(res_loaded[s], (i * (UNROLL2 // 4) + (j - AT_X2 + 1) // 4 + 1) * 16)
                    pool.tensor_tensor(x_res[s], x_res[s], bo_all, ALU.add).then_inc(res_ready, 1)
                if attend.live(i, j, AT_SEND):
                    n, g, q = i * UNROLL2 + j - AT_SEND, (j - AT_SEND) // PG % 2, (j - AT_SEND) % PG
                    if q == 0:
                        pool.wait_ge(rows_ready, n + PG)
                        carry_wait()
                    for k in range(TOPK):
                        pool.indirect_dma_start(sorted_rows, bass.IndirectOffsetOnAxis(ap=index[g][:, k, q:q + 1], axis=0),
                                                rows[g][:, q, k, :], None).then_inc(scattered[g], 16)

            attend(pool, AT_SEND, expand_step)
            def send_step(i, j):
                if not experts.live(i, j, 4):
                    return
                t, s = i * UNROLL3 + j - 4, (j - 4) % 4
                pool.wait_ge(y_ready, t + 1)
                carry_wait()
                pool.indirect_dma_start(expert_out, bass.IndirectOffsetOnAxis(ap=y_index[s][:, :], axis=0),
                                        y_out[s], None).then_inc(y_sent[s], 16)

            experts(pool, 4, send_step)

        @block.vector
        def _(dve):
            dve.wait_ge(const_loaded, N_CONST)
            dve.tensor_copy(ident_r[:, :], ident)
            dve.tensor_copy(tri_r[:, :], tri)
            dve.tensor_copy(ones_r[:, :], ones)
            dve.tensor_scalar(either[:, PG, :], const(C_RANK, E), 0.0, None, ALU.mult)
            dve.tensor_copy(base[:, :], const(C_REGION, E))
            dve.tensor_copy(dest[:, :, :], const(C_DEST, PG * TOPK).rearrange("p (q k) -> p q k", q=PG))
            dve.wait_ge(bo_done, 1)
            dve.tensor_tensor(bo_sb[:, :], bank[0][0:1, 0:D], bo_sb[:, :], ALU.add)
            dve.wait_ge(tanh_ready, 1)
            dve.tensor_scalar(wo_sb[:, :], wo_sb[:, :], tanh_gate[:, 0:1], None, ALU.mult)
            dve.drain()
            dve.tensor_scalar(bo_sb[:, :], bo_sb[:, :], tanh_gate[0:1, 0:1], None, ALU.mult).then_inc(consts_ready, 1)

            def project_step(i, j):
                n = i * UNROLL1 + j
                if project.live(i, j):
                    s = j % 4
                    dve.wait_ge(x_loaded[s], (i * (UNROLL1 // 4) + j // 4 + 1) * 16)
                    for q in range(PG):
                        dve.bn_stats(stats[:, q, :], x_in[s][:, q * D:q * D + D])
                    dve.drain()
                    for q in range(PG):
                        last = dve.bn_aggr(mv[:, q, :], stats[:, q, :])
                    last.then_inc(var_ready, 1)
                if project.live(i, j):
                    s = j % 4
                    dve.wait_ge(std_ready, n + 1)
                    dve.reciprocal(rstd[:, :], std[:, :])
                    dve.drain()
                    for q in range(PG):
                        last = dve.tensor_scalar(x_in[s][:, q * D:q * D + D], x_in[s][:, q * D:q * D + D],
                                                 mv[:, q, 0:1], rstd[:, q:q + 1], ALU.subtract, ALU.mult)
                    last.then_inc(xn_ready, 1)
                if project.live(i, j, 2):
                    dve.wait_ge(v_done, n - 1)
                    for h in range(2):
                        last = dve.tensor_copy(v_all[:, bass.ds((n - 2) * 2 * D * PG + h * 512, 512)], bank[6 + h][:, :])
                    last.then_inc(v_copied, 1)

            project(dve, 2, project_step)

            def norm(stage, i, j, g):
                if stage == 0:
                    for q in range(PG):
                        dve.bn_aggr(mv[:, q, :], stats[:, q, :])
                elif stage == 1:
                    dve.tensor_scalar(var[:, :], mv[:, :, 1], EPS, None, ALU.add)
                elif stage == 2:
                    dve.tensor_scalar(newton[:, :].bitcast(U32), var[:, :].bitcast(U32), 1, None, ALU.logical_shift_right)
                elif stage == 3:
                    dve.tensor_scalar(rstd[:, :].bitcast(I32), newton[:, :].bitcast(I32), -1.0, float(MAGIC), ALU.mult, ALU.add)
                elif stage == 13:
                    if attend.reached(i, j, AT_NORM + 2 + 2 * PG):
                        dve.wait_ge(rows_copied, group_of(i, j, AT_NORM + 2) - 1)
                    for q in range(PG):
                        last = dve.tensor_scalar(xn2g[g][:, q, :], x2g[g][:, q, :], mv[:, q, 0:1], rstd[:, q:q + 1], ALU.subtract, ALU.mult)
                    last.then_inc(xn2_ready, 1)
                elif stage % 3 == 1:
                    dve.tensor_tensor(newton[:, :], rstd[:, :], rstd[:, :], ALU.mult)
                elif stage % 3 == 2:
                    dve.scalar_tensor_tensor(newton[:, :], newton[:, :], -0.5, var[:, :], ALU.mult, ALU.mult)
                else:
                    dve.scalar_tensor_tensor(rstd[:, :], newton[:, :], 1.5, rstd[:, :], ALU.add, ALU.mult)

            rank = const(C_RANK, E).unsqueeze(1).to_broadcast([P, PG, E])
            spread = lambda v: v[:, :].unsqueeze(2).to_broadcast([P, PG, E])

            def choose(stage, g):
                k = stage // 6
                left, top = (logits[g][:, :, :], best) if k == 0 else (rest[:, :, :], second)
                if stage % 6 == 0:
                    dve.tensor_reduce(top[:, :], left, AX.X, ALU.max)
                elif stage % 6 == 1:
                    dve.tensor_tensor(work[:, 0], left, spread(top), ALU.is_equal)
                elif stage % 6 == 2:
                    dve.tensor_tensor(work[:, 0], work[:, 0], rank, ALU.mult)
                elif stage % 6 == 3:
                    dve.tensor_reduce(picked[:, :], work[:, 0], AX.X, ALU.max)
                elif stage % 6 == 4:
                    dve.tensor_tensor(chosen[:, k], rank, spread(picked), ALU.is_equal)
                elif k == 0:
                    dve.scalar_tensor_tensor(rest[:, :, :], chosen[:, 0], BELOW_ALL, left, ALU.mult, ALU.add)
                else:
                    dve.tensor_tensor(either[:, 0:PG, :], chosen[:, 0], chosen[:, 1], ALU.add)
                    dve.tensor_tensor(gap[:, :], second[:, :], best[:, :], ALU.subtract).then_inc(gap_ready, 1)

            def place_rows(stage, i, j):
                if stage == 0:
                    dve.tensor_tensor(place[:, :, :], aux[:, AUX_R:AUX_R + PG * E].rearrange("p (q e) -> p q e", e=E),
                                      base[:, :].unsqueeze(1).to_broadcast([P, PG, E]), ALU.add)
                    dve.wait_ge(ratio_ready, group_of(i, j, AT_PLACE) + 1)
                    dve.tensor_scalar(share[:, :], ratio[:, :], 1.0, None, ALU.add)
                elif stage == 1:
                    dve.tensor_tensor(base[:, :], aux[:, AUX_T:AUX_T + E], base[:, :], ALU.add).then_inc(mid_read, 1)
                    for k in range(TOPK):
                        dve.tensor_tensor(work[:, k], chosen[:, k], place[:, :, :], ALU.mult)
                    dve.reciprocal(share[:, :], share[:, :])
                elif stage == 2:
                    dve.tensor_reduce(place_of[:, :, :], work[:, :, :, :], AX.X, ALU.add)
                    dve.tensor_scalar(share[:, :], share[:, :], tanh_gate[:, 1:2], None, ALU.mult)

            def fill_rows(stage, i, j):
                g = (j - AT_PLACE - 1) // PG % 2
                if stage == 0:
                    if attend.reached(i, j, AT_PLACE + 1 + 2 * PG):
                        dve.wait_ge(scattered[g], (i * (UNROLL2 // (2 * PG)) + (j - AT_PLACE - 1) // (2 * PG)) * PG * TOPK * 16)
                    dve.wait_ge(rows_copied, group_of(i, j, AT_PLACE + 1) + 1)
                    dve.tensor_copy(index[g][:, :, :], place_of[:, :, :])
                    dve.tensor_copy(rows[g][:, :, :, D], dest[:, :, :])
                    dve.tensor_copy(rows[g][:, :, 0, D + 1], share[:, :])
                    dve.tensor_tensor(rows[g][:, :, 1, D + 1], share[:, :], ratio[:, :], ALU.mult).then_inc(rows_ready, PG)
                elif stage == 1:
                    dve.tensor_scalar(dest[:, :, :], dest[:, :, :], float(PG * P * TOPK), None, ALU.add)

            def group_work(i, j):
                at = lambda lag: (j - lag) % PG == 0 and attend.live(i, j, lag)
                slot = lambda lag: (j - lag) // PG % 2
                if at(AT_CHOOSE):
                    dve.wait_ge(end_read, m_or_last(i * UNROLL2 + j) - AT_TURN)
                if not any(at(lag) for lag in (AT_NORM, AT_NORM + 1, AT_NORM + 2, AT_CHOOSE, AT_CHOOSE + 1, AT_CHOOSE + 2,
                                               AT_PLACE, AT_PLACE + 1)):
                    return
                stages = 5 if at(AT_NORM) or at(AT_NORM + 1) else 4
                for stage in range(stages):
                    for part in range(3):
                        if at(AT_NORM + part):
                            norm(5 * part + stage, i, j, slot(AT_NORM + part))
                    for quarter in range(3):
                        if at(AT_CHOOSE + quarter) and stage < 4:
                            choose(4 * quarter + stage, slot(AT_CHOOSE + quarter))
                    if at(AT_PLACE):
                        place_rows(stage, i, j)
                    if at(AT_PLACE + 1):
                        fill_rows(stage, i, j)
                    if stage < stages - 1 or not attend.live(i, j, 3):
                        dve.drain()

            def attend_step(i, j):
                m = i * UNROLL2 + j
                if attend.live(i, j):
                    s = j % 2
                    dve.wait_ge(scores_done, m + 1)
                    if attend.reached(i, j, 2):
                        dve.wait_ge(shifted, m - 1)
                    for half in range(2):
                        last = dve.tensor_reduce(neg_max[s][:, half * 8:half * 8 + 8],
                                                 scores[s][half][:, :].rearrange("p (h k) -> p h k", k=S), AX.X, ALU.max, negate=True)
                    last.then_inc(max_ready, 1)
                x2_live, turn_live = attend.live(i, j, AT_X2), attend.live(i, j, AT_TURN)
                place_live = (j - AT_PLACE) % PG == 0 and attend.live(i, j, AT_PLACE)
                if x2_live or turn_live or place_live:
                    dve.wait_ge(mid_done, m_or_last(m) - 4)
                n, s, g, q = m - AT_X2, (j - AT_X2) % 4, (j - AT_X2) // PG % 2, (j - AT_X2) % PG
                if x2_live:
                    dve.wait_ge(res_ready, n + 1)
                    if q == 0 and attend.reached(i, j, AT_X2 + 2 * PG):
                        dve.wait_ge(x2_copied, n - PG)
                    dve.tensor_tensor(x2g[g][:, q, :], aux[:, AUX_O:AUX_O + D], x_res[s], ALU.add).then_inc(x2_ready, 1)
                if turn_live:
                    last = dve.tensor_copy(xn2_t[(j - AT_TURN) % 2][:, :], aux[:, AUX_X:AUX_X + D])
                    if not place_live:
                        last.then_inc(mid_read, 1)
                if x2_live and (q == PG - 1 or isinstance(i, int)):
                    dve.drain()
                    last = dve.bn_stats(stats[:, q, :], x2g[g][:, q, :])
                    if not turn_live and not place_live:
                        last.then_inc(mid_read, 1)
                    dve.drain()
                group_work(i, j)
                if x2_live and not (q == PG - 1 or isinstance(i, int)):
                    dve.bn_stats(stats[:, q, :], x2g[g][:, q, :])
                if attend.live(i, j, 3):
                    n, s = m - 3, (j - 3) % 2
                    dve.wait_ge(av_done, n + 1)
                    dve.reciprocal(rsum[:, :], bank[6][:, P:2 * P])
                    dve.drain()
                    dve.tensor_tensor(o_t[s][:, :], bank[6][:, 0:P], rsum[:, :], ALU.mult).then_inc(o_ready, 1)

            attend(dve, AT_SEND, attend_step)

            dve.tensor_copy(first_pad[:, :], base[:, :]).then_inc(pads_ready, 1)
            dve.tensor_tensor(count[:, :], base[:, :], const(C_REGION, E), ALU.subtract)
            dve.drain()
            dve.tensor_scalar(count[:, :], count[:, :], float(P - 1), None, ALU.add)
            dve.drain()
            dve.tensor_copy(count_i[:, :], count[:, :])
            dve.drain()
            dve.tensor_scalar(count_i[:, :], count_i[:, :], 7, None, ALU.logical_shift_right)
            dve.drain()
            dve.tensor_copy(tiles_of[:, :], count_i[:, :])
            dve.drain()
            dve.tensor_scalar(skip[:, :], tiles_of[:, :], -float(P), float(REGION), ALU.mult, ALU.add)
            src = tiles_of
            for n, step in enumerate((1, 2, 4)):
                dst = upto[n % 2]
                dve.tensor_copy(dst[:, 0:step], src[:, 0:step])
                dve.tensor_tensor(dst[:, step:E], src[:, step:E], src[:, 0:E - step], ALU.add)
                dve.drain()
                src = dst
            tile = const_sb[0:1, C_TILE:C_TILE + TILES]
            dve.tensor_tensor(passed, tile.unsqueeze(2).to_broadcast([1, TILES, E]),
                              src[0:1, :].unsqueeze(1).to_broadcast([1, TILES, E]), ALU.is_ge)
            dve.drain()
            dve.tensor_tensor(skipped, passed, skip[0:1, :].unsqueeze(1).to_broadcast([1, TILES, E]), ALU.mult)
            dve.tensor_reduce(tile_f[:, 0, :], passed, AX.X, ALU.add)
            dve.drain()
            dve.tensor_reduce(tile_f[:, 1, :], skipped, AX.X, ALU.add)
            dve.tensor_scalar(tile_expert[:, :], tile_f[:, 0, :], float(E - 1), None, ALU.min)
            dve.drain()
            dve.scalar_tensor_tensor(tile_f[:, 1, :], tile, float(P), tile_f[:, 1, :], ALU.mult, ALU.add)
            dve.drain()
            dve.tensor_copy(tile_row[:, :], tile_f[:, 1, :]).then_inc(table_ready, 1)
            for s in range(2):
                dve.memset(hidden[s][:, H:HP], 0.0)
            for e in range(E):
                cols = slice(e * 2 * H, (e + 1) * 2 * H)
                dve.wait_ge(high_ready, e + 1)
                dve.tensor_tensor(w13_rest[:, cols], w13_sb[:, cols], w13_high[:, cols], ALU.subtract).then_inc(rest_ready, 1)

            def expert_step(i, j):
                t = i * UNROLL3 + j
                if experts.live(i, j):
                    dve.wait_ge(row_copied, t + 1)
                    dve.tensor_tensor(xt_rest[j % 2][:, :], bank[0][:, 0:D], xt_high[j % 2][:, :], ALU.subtract).then_inc(row_rest, 1)
                if experts.live(i, j, 1):
                    s, s4 = (j - 1) % 2, (j - 1) % 4
                    dve.wait_ge(gated_ready, t)
                    if experts.reached(i, j, 3):
                        dve.wait_ge(hidden_turned, t - 2)
                    dve.scalar_tensor_tensor(hidden[s][:, 0:H], gated[s], row_in[s4][:, D + 1:D + 2], bank[3 + s][:, 0:H],
                                             ALU.mult, ALU.mult)
                    if experts.reached(i, j, 5):
                        use = i * (UNROLL3 // 4) + (j - 1) // 4
                        dve.wait_ge(y_sent[s4], use * 16)
                    dve.tensor_copy(y_index[s4][:, :], row_in[s4][:, D:D + 1]).then_inc(hidden_ready, 1)
                if experts.live(i, j, 3):
                    s, s4 = (j - 3) % 2, (j - 3) % 4
                    dve.wait_ge(down_done, t - 2)
                    dve.tensor_copy(y_out[s4], bank[6 + s][:, 0:D]).then_inc(y_ready, 1)

            experts(dve, 3, expert_step)

            def sum_step(i, j):
                s, n, u = j % 4, i * UNROLL4 + j, i * (UNROLL4 // 4) + j // 4
                dve.wait_ge(y_loaded[s], (u + 1) * 16)
                y = y_in[s].rearrange("p (n k d) -> p n k d", n=PG, k=TOPK)
                x2 = qx_all[:, bass.ds(n * PG * D, PG * D)].rearrange("p (n d) -> p n d", d=D)
                dve.tensor_tensor(y[:, :, 0, :], y[:, :, 0, :], y[:, :, 1, :], ALU.add)
                dve.drain()
                dve.tensor_tensor(x2, x2, y[:, :, 0, :], ALU.add).then_inc(sum_ready, 1)

            combine(dve, 0, sum_step)

        @block.scalar
        def _(act):
            act.wait_ge(const_loaded, N_CONST)
            act.activation(tanh_gate[:, :], gate_sb[:, :], ACT.Tanh).then_inc(tanh_ready, 1)

            def project_step(i, j):
                n = i * UNROLL1 + j
                if project.live(i, j):
                    act.wait_ge(var_ready, n + 1)
                    act.activation(std[:, :], mv[:, :, 1], ACT.Sqrt, bias=const(C_EPS)).then_inc(std_ready, 1)
                if project.live(i, j, 1):
                    s = (j - 1) % 2
                    act.wait_ge(xt_done, n)
                    if project.reached(i, j, 3):
                        act.wait_ge(q_done, n - 2)
                    act.copy(xn_t[s], bank[s][:, :]).then_inc(xt_copied, 1)
                if project.live(i, j, 2):
                    s = j % 2
                    for store, out_bank, bias, done, copied in ((k_all, bank[2 + s], 2, k_done, k_copied), (qx_all, bank[4 + s], 0, q_done, q_copied)):
                        act.wait_ge(done, n - 1)
                        for t in range(2):
                            dst = store[:, bass.ds((n - 2) * 2 * S * PG, 2 * S * PG)].rearrange("p (q t k) -> p q t k", q=PG, t=2)
                            last = act.activation(dst[:, :, t, :], out_bank[:, 256 * t:256 * t + 256].rearrange("p (q k) -> p q k", q=PG),
                                                  ACT.Identity, bias=bias_sb[:, bias + t:bias + t + 1])
                        last.then_inc(copied, 1)

            project(act, 2, project_step)
            act.wait_ge(bo_spread, 1)
            act.copy(bo_all, aux[:, AUX_O:AUX_O + D]).then_inc(bo_all_ready, 1)

            def attend_step(i, j):
                m = i * UNROLL2 + j
                if (j - AT_PLACE) % PG == 0 and attend.live(i, j, AT_PLACE):
                    act.wait_ge(gap_ready, group_of(i, j, AT_PLACE) + 1)
                    act.activation(ratio[:, :], gap[:, :], ACT.Exp).then_inc(ratio_ready, 1)
                if attend.live(i, j, 1):
                    n, s = m - 1, (j - 1) % 2
                    act.wait_ge(shifted, n + 1)
                    if attend.reached(i, j, 3):
                        act.wait_ge(t_done[1], n - 1)
                    for half in range(2):
                        last = act.activation(probs[s][:, half * 512:half * 512 + 512], scores[s][half][:, :], ACT.Exp, scale=HD ** -0.5)
                    last.then_inc(probs_ready, 1)
                if attend.live(i, j, 2):
                    n, s = m - 2, j % 2
                    act.wait_ge(t_done[0], n + 1)
                    if attend.reached(i, j, 4):
                        act.wait_ge(av_done, n - 1)
                    act.copy(probs_t[s][:, 0:512], bank[4][:, :]).then_inc(t_copied[0], 1)
                    act.wait_ge(t_done[1], n + 1)
                    act.copy(probs_t[s][:, 512:1024], bank[5][:, :]).then_inc(t_copied[1], 1)
                if attend.live(i, j, AT_TURN):
                    act.wait_ge(end_done, m - AT_TURN + 1)
                    g, q = (j - AT_TURN) // PG % 2, (j - AT_TURN) % PG
                    act.copy(logits[g][:, q, :], aux[:, AUX_L:AUX_L + E]).then_inc(end_read, 1)
                if attend.live(i, j, AT_X2 + 1):
                    n, g, q = m - AT_X2 - 1, (j - AT_X2 - 1) // PG % 2, (j - AT_X2 - 1) % PG
                    act.wait_ge(x2_ready, n + 1)
                    act.copy(qx_all[:, bass.ds(n * D, D)], x2g[g][:, q, :]).then_inc(x2_copied, 1)
                if (j - AT_COPY) % PG == 0 and attend.live(i, j, AT_COPY):
                    g = (j - AT_COPY) // PG % 2
                    if attend.reached(i, j, AT_COPY + 2 * PG):
                        act.wait_ge(scattered[g], (i * (UNROLL2 // (2 * PG)) + (j - AT_COPY) // (2 * PG)) * PG * TOPK * 16)
                    act.wait_ge(xn2_ready, group_of(i, j, AT_COPY) + 1)
                    act.copy(rows[g][:, :, :, 0:D], xn2g[g][:, :, :].unsqueeze(2).to_broadcast([P, PG, TOPK, D])).then_inc(rows_copied, 1)

            attend(act, AT_SEND, attend_step)

            act.wait_ge(w13_loaded, 16)
            act.wait_ge(values_ready, 2 * PAIRS)
            for e in range(E):
                cols = slice(e * 2 * H, (e + 1) * 2 * H)
                act.copy(w13_high[:, cols], w13_sb[:, cols]).then_inc(high_ready, 1)

            def expert_step(i, j):
                t = i * UNROLL3 + j
                if experts.live(i, j):
                    s = j % 2
                    act.wait_ge(row_turned, t + 1)
                    if experts.reached(i, j, 2):
                        act.wait_ge(up_done, t - 1)
                    act.copy(xt_high[s][:, :], bank[0][:, 0:D]).then_inc(row_copied, 1)
                if experts.live(i, j, 1):
                    s = (j - 1) % 2
                    act.wait_ge(up_done, t)
                    if experts.reached(i, j, 3):
                        act.wait_ge(hidden_ready, t - 2)
                    act.activation(gated[s], bank[1 + s][:, 0:H], ACT.Silu).then_inc(gated_ready, 1)
                if experts.live(i, j, 2):
                    s = j % 2
                    act.wait_ge(hidden_turned, t - 1)
                    if experts.reached(i, j, 4):
                        act.wait_ge(down_done, t - 3)
                    act.copy(hidden_t[s], bank[5][:, 0:HP]).then_inc(hidden_copied, 1)

            experts(act, 2, expert_step)

            def store_step(i, j):
                n = i * UNROLL4 + j
                act.wait_ge(sum_ready, n + 1)
                act.dma_start(out_v[:, bass.ds(n * PG, PG), :],
                              qx_all[:, bass.ds(n * PG * D, PG * D)].rearrange("p (n d) -> p n d", d=D)).then_inc(stored, 16)

            combine(act, 0, store_step)

        @block.tensor
        def _(pe):
            pe.wait_ge(const_loaded, N_CONST)
            pe.matmul(bank[0][0:1, 0:D], bv_sb[:, :], wo_sb[:, :], start=True, stop=True).then_inc(bo_done, 1)
            pe.wait_ge(consts_ready, 1)

            def project_step(i, j):
                m = i * UNROLL1 + j
                if project.live(i, j, 1):
                    s = (j - 1) % 2
                    pe.wait_ge(xn_ready, m)
                    if project.reached(i, j, 3):
                        pe.wait_ge(xt_copied, m - 2)
                    for q in range(PG):
                        last = pe.transpose(bank[s][:, q * D:q * D + D], x_in[(j - 1) % 4][:, q * D:q * D + D], ident)
                    last.then_inc(xt_done, 1)
                if project.live(i, j, 2):
                    n, s, s4, u = m - 2, j % 2, (j - 2) % 4, i * (UNROLL1 // 4) + (j - 2) // 4
                    pe.wait_ge(c_loaded[s4], (u + 1) * 16)
                    for src, w0, out_bank, ready, free, done in ((c_t[s4], D, bank[2 + s], None, k_copied, k_done),
                                                                 (xn_t[s], 0, bank[4 + s], xt_copied, q_copied, q_done)):
                        if ready is not None:
                            pe.wait_ge(ready, n + 1)
                        if project.reached(i, j, 4):
                            pe.wait_ge(free, n - 1)
                        rhs = src.rearrange("p (q b k) -> p b q k", q=PG, b=2)
                        for t in range(2):
                            for half in range(2):
                                for b in range(2):
                                    c = 64 * half + 32 * b
                                    f = w0 + 64 * half + 32 * t
                                    last = pe.matmul(out_bank[c:c + 32, 256 * t:256 * t + 256], wqkv_sb[:, f:f + 32], rhs[:, b],
                                                     start=True, stop=True)
                        last.then_inc(done, 1)
                    if project.reached(i, j, 3):
                        pe.wait_ge(v_copied, n)
                    for q in range(PG):
                        for b in range(2):
                            for h in range(2):
                                last = pe.matmul(bank[6 + q // 2][64 * h:64 * h + 64, (q % 2 * 2 + b) * D:(q % 2 * 2 + b + 1) * D],
                                                 c_t[s4][:, (2 * q + b) * S:(2 * q + b + 1) * S], wqkv_sb[:, 2 * D:3 * D],
                                                 start=True, stop=True)
                    last.then_inc(v_done, 1)

            project(pe, 2, project_step)
            pe.wait_ge(k_copied, GROUPS)
            pe.wait_ge(q_copied, GROUPS)
            pe.wait_ge(v_copied, GROUPS)
            pe.matmul(aux[:, AUX_O:AUX_O + D], ones[0:1, :], bo_sb[0:1, :], start=True, stop=True).then_inc(bo_spread, 1)
            pe.wait_ge(bo_all_ready, 1)

            def attend_step(i, j):
                m = i * UNROLL2 + j
                if attend.live(i, j):
                    s = j % 2
                    pe.wait_ge(operands_ready, 2 * m + 2)
                    if attend.reached(i, j, 2):
                        pe.wait_ge(probs_ready, m - 1)
                    for t in range(2):
                        for half in range(2):
                            last = pe.matmul(scores[s][half][:, 256 * t:256 * t + 256],
                                             q_blk[s][64 * half:64 * half + 64, t, :, :],
                                             k_mask[s][64 * half:64 * half + 64, t, :, :],
                                             start=t == 0, stop=t == 1, skip_group_check=True)
                    last.then_inc(scores_done, 1)
                x2_live, turn_live = attend.live(i, j, AT_X2), attend.live(i, j, AT_TURN)
                place_live = (j - AT_PLACE) % PG == 0 and attend.live(i, j, AT_PLACE)
                if x2_live or turn_live or place_live:
                    if attend.reached(i, j, AT_TURN + 1):
                        pe.wait_ge(end_read, m_or_last(m) - AT_TURN)
                    if attend.reached(i, j, AT_X2 + 1):
                        pe.wait_ge(mid_read, m_or_last(m) - AT_X2)
                    if x2_live:
                        pe.wait_ge(o_ready, m - AT_X2 + 1)
                    if turn_live:
                        g, q = (j - AT_TURN) // PG % 2, (j - AT_TURN) % PG
                        if q == 0:
                            pe.wait_ge(xn2_ready, group_of(i, j, AT_TURN) + 1)
                        last = pe.transpose(aux[:, AUX_X:AUX_X + D], xn2g[g][:, q, :], ident)
                    if x2_live:
                        s = (j - AT_X2) % 2
                        last = pe.matmul(aux[:, AUX_O:AUX_O + D], o_t[s][:, :], wo_sb[:, :], start=True, stop=True)
                    if place_live:
                        pe.wait_ge(gap_ready, group_of(i, j, AT_PLACE) + 1)
                        pe.matmul(aux[:, AUX_R:AUX_T + E], tri_r[:, :], either[:, :, :], start=True, stop=False, skip_group_check=True)
                        for q in range(PG):
                            last = pe.matmul(aux[:, AUX_R + (q + 1) * E:AUX_T + E], ones_r[:, :],
                                             either[:, q:q + 1, :].to_broadcast([P, PG - q, E]), start=False, stop=q == PG - 1,
                                             skip_group_check=True)
                    last.then_inc(mid_done, 1)
                if attend.live(i, j, 1):
                    n, s = m - 1, (j - 1) % 2
                    pe.wait_ge(max_ready, n + 1)
                    for half in range(2):
                        last = pe.matmul(scores[s][half][:, :], ident_r[:, :],
                                         neg_max[s][:, half * 8:half * 8 + 8].unsqueeze(2).to_broadcast([P, 8, S]),
                                         start=False, stop=True, skip_group_check=True)
                    last.then_inc(shifted, 1)
                if attend.live(i, j, 2):
                    n, s = m - 2, (j - 2) % 2
                    pe.wait_ge(probs_ready, n + 1)
                    for half in range(2):
                        if attend.reached(i, j, 3):
                            pe.wait_ge(t_copied[half], n)
                        for c in range(4):
                            last = pe.transpose(bank[4 + half][:, c * P:c * P + P], probs[s][:, half * 512 + c * P:half * 512 + c * P + P], ident)
                        last.then_inc(t_done[half], 1)
                if attend.live(i, j, 3):
                    n, s = m - 3, (j - 3) % 2
                    pe.wait_ge(values_ready, 2 * n + 2)
                    if attend.reached(i, j, 4):
                        pe.wait_ge(o_ready, n)
                    for half in range(2):
                        pe.wait_ge(t_copied[half], n + 1)
                    for r in range(2):
                        for b in range(2):
                            for g in range(4):
                                at = b * 256 + g * 64 + r * 32
                                pe.matmul(bank[6][32 * g:32 * g + 32, b * S:b * S + S], v_blk[s][:, at:at + 32],
                                          probs_t[s][:, (2 * g + r) * P + b * S:(2 * g + r) * P + b * S + S],
                                          start=r == 0 and b == 0, stop=r == 1, skip_group_check=True)
                    for r in range(2):
                        for g in range(4):
                            last = pe.matmul(bank[6][32 * g:32 * g + 32, P:2 * P], const(C_SUM + 32 * r, 32),
                                             probs_t[s][:, (2 * g + r) * P:(2 * g + r) * P + P],
                                             start=False, stop=r == 1, skip_group_check=True)
                    last.then_inc(av_done, 1)
                if attend.live(i, j, AT_TURN):
                    pe.wait_ge(mid_read, m - 4)
                    pe.matmul(aux[:, AUX_L:AUX_L + E], xn2_t[(j - AT_TURN) % 2][:, :], wgate_sb[:, :], start=True, stop=True).then_inc(end_done, 1)

            attend(pe, AT_SEND, attend_step)
            pe.wait_ge(table_ready, 1)
            pe.wait_ge(rest_ready, E)
            pe.wait_ge(w2_loaded, 16)
            of_expert = lambda w, e, k: w[:, :].rearrange("p (e k h) -> p e k h", e=E, k=2)[:, bass.ds(e, 1), k, :].rearrange("p e h -> p (e h)")
            w2_of = lambda c, e: w2_sb[:, :].rearrange("p (c e d) -> p c e d", c=CHUNKS, e=E)[:, c, bass.ds(e, 1), :].rearrange("p e d -> p (e d)")
            loaded = [None] * 4

            def load_expert(t):
                return nc.s_assert_within(pe.value_load(tile_expert[0:1, bass.ds(t, 1)]), 0, E - 1,
                                          skip_runtime_bounds_check_because="the table's entries are limited to E - 1")

            def expert_step(i, j):
                t = i * UNROLL3 + j
                if experts.live(i, j, 1):
                    loaded[j % 4] = load_expert(t - 1)
                if experts.live(i, j, 3) and j < 2:
                    loaded[(j - 2) % 4] = load_expert(t - 3)
                if experts.live(i, j, 1):
                    s = (j - 1) % 2
                    pe.wait_ge(row_rest, t)
                    for k in range(2):
                        for n, (x_part, w_part) in enumerate(((xt_high, w13_high), (xt_high, w13_rest), (xt_rest, w13_high))):
                            last = pe.matmul(bank[1 + 2 * k + s][:, 0:H], x_part[s][:, :], of_expert(w_part, loaded[j % 4], k),
                                             start=n == 0, stop=n == 2)
                    last.then_inc(up_done, 1)
                if experts.live(i, j):
                    u = i * (UNROLL3 // 4) + j // 4
                    pe.wait_ge(row_loaded[j % 4], (u + 1) * 16)
                    pe.transpose(bank[0][:, 0:D], row_in[j % 4][:, 0:D], ident).then_inc(row_turned, 1)
                if experts.live(i, j, 2):
                    s = j % 2
                    pe.wait_ge(hidden_ready, t - 1)
                    if experts.reached(i, j, 3):
                        pe.wait_ge(hidden_copied, t - 2)
                    for c in range(CHUNKS):
                        last = pe.transpose(bank[5][:, c * P:c * P + P], hidden[s][:, c * P:c * P + P], ident)
                    last.then_inc(hidden_turned, 1)
                if experts.live(i, j, 3):
                    s = (j - 3) % 2
                    if not experts.live(i, j, 2):
                        pe.wait_ge(hidden_copied, t - 2)
                    if experts.reached(i, j, 5) and not experts.live(i, j, 1):
                        pe.wait_ge(y_ready, t - 4)
                    for c in range(CHUNKS):
                        last = pe.matmul(bank[6 + s][:, 0:D], hidden_t[s][:, c * P:c * P + P],
                                         w2_of(c, loaded[(j - 2) % 4]), start=c == 0, stop=c == CHUNKS - 1)
                    last.then_inc(down_done, 1)

            experts(pe, 3, expert_step)


def constants():
    import numpy as np
    p = np.arange(P)
    columns = [np.eye(P), np.triu(np.ones((P, P)), 1), np.ones((P, P)),
               (p // HD % QUAD)[:, None] == np.arange(QUAD)[None],
               (p // 32 % 2)[:, None] == np.arange(2)[None],
               (p // S)[:, None] == np.arange(2)[None],
               (p // S)[:, None] + 2 * (np.arange(64) // 32)[None] == (np.arange(64) % 32 // HD)[None],
               np.full((P, 1), EPS),
               np.tile(E - np.arange(E), (P, 1)),
               np.tile(REGION * np.arange(E), (P, 1)),
               TOPK * (P * (np.arange(PG * TOPK) // TOPK)[None] + p[:, None]) + (np.arange(PG * TOPK) % TOPK)[None],
               TRASH + P * np.arange(2 * E)[None] + p[:, None],
               np.tile(np.arange(TILES), (P, 1))]
    return np.concatenate([np.asarray(c, np.float32) for c in columns], axis=1)


def kernel(**inputs):
    import numpy as np
    import concourse.bacc as bacc
    from concourse import mybir
    from concourse.bass_utils import run_bass_kernel_spmd

    p = np.arange(P)
    feature = [64 * (p // 64) + 32 * t + p % 32 for t in range(2)]
    bq, bkv = inputs["L0_xattn_bq"], inputs["L0_xattn_bkv"]
    w1, w3, w2 = inputs["L0_ffn_w1"], inputs["L0_ffn_w3"], inputs["L0_ffn_w2"]
    w13 = np.concatenate([w1.transpose(2, 0, 1), w3.transpose(2, 0, 1)], axis=2).reshape(D, E * 2 * H)
    w2p = np.pad(w2.transpose(2, 0, 1), ((0, HP - H), (0, 0), (0, 0)))
    w2p = w2p.reshape(CHUNKS, P, E * D).transpose(1, 0, 2).reshape(P, CHUNKS * E * D)
    arrays = {
        "x": inputs["x"],
        "ctx": inputs["ctx_1024"].reshape(TOKENS, D).T,
        "consts": constants(),
        "qk_bias": np.stack([bq[feature[0]], bq[feature[1]], bkv[:D][feature[0]], bkv[:D][feature[1]]], axis=1),
        "gates": np.concatenate([np.broadcast_to(inputs["g_xattn"], (P, 1)), np.broadcast_to(inputs["g_ffn"], (P, 1))], axis=1),
        "bv": bkv[D:].reshape(P, 1),
        "bo": inputs["L0_xattn_bo"].reshape(1, D),
        "w_qkv": np.concatenate([inputs["L0_xattn_Wq"], inputs["L0_xattn_Wkv"]], axis=1),
        "w_o": inputs["L0_xattn_Wo"],
        "w_gate": inputs["L0_ffn_gate_w"].T,
        "w13": w13,
        "w2": w2p,
    }
    arrays = {n: np.ascontiguousarray(a) for n, a in arrays.items()}
    nc = bacc.Bacc("TRN2", target_bir_lowering=False, num_devices=1)
    args = [nc.dram_tensor("in_" + n, a.shape, mybir.dt.from_np(a.dtype), kind="ExternalInput").ap() for n, a in arrays.items()]
    out = nc.dram_tensor("out", (B, S, D), mybir.dt.from_np(np.dtype("float32")), kind="ExternalOutput").ap()
    build(nc, *args, out)
    r = run_bass_kernel_spmd(nc, [{"in_" + n: a for n, a in arrays.items()}], core_ids=[0])
    return r.results[0]["out"]
```
